# Optimizing a Trainium2 kernel written in Bass

```python
import numpy as np
import jax
import jax.numpy as jnp

def _softmax(x, axis=-1):
    return jax.nn.softmax(x, axis=axis)

def _gelu(x):
    return jax.nn.gelu(x, approximate=True)

def _silu(x):
    return jax.nn.silu(x)

def _sigmoid(x):
    return jax.nn.sigmoid(x)

def _layernorm(x, axis=-1, eps=1e-05):
    m = jnp.mean(x, axis=axis, keepdims=True)
    v = jnp.var(x, axis=axis, keepdims=True)
    return (x - m) / jnp.sqrt(v + eps)

def _scatter_add(tgt, idx, src, axis=0):
    return tgt.at[idx].add(src)

def _segment_sum(src, seg, n):
    return jax.ops.segment_sum(src, seg, n)
kernel_name = 'mk_seq_preln_d1_jaxref_r8_251525'

def setup_inputs(seed: int=0):
    np.random.seed(seed)
    _w = jnp.asarray

    def _L0_attn_setup():
        import jax, jax.numpy as jnp
        import numpy as np
        B, S, IN_DIM, D_MODEL, NUM_HEADS = (4, 256, 128, 128, 16)
        HEAD_DIM = D_MODEL // NUM_HEADS
        CAUSAL = True
        NEG = -9000000000000000.0

        def _xavier(key, shape):
            fan_out, fan_in = shape
            limit = (6.0 / (fan_in + fan_out)) ** 0.5
            return jax.random.uniform(key, shape, jnp.float32, -limit, limit)
        key = jax.random.key(seed)
        ks = jax.random.split(key, 5)
        x = jax.random.normal(ks[0], (B, S, IN_DIM), jnp.float32)
        Wq = _xavier(ks[1], (D_MODEL, IN_DIM))
        Wk = _xavier(ks[2], (D_MODEL, IN_DIM))
        Wv = _xavier(ks[3], (D_MODEL, IN_DIM))
        Wo = _xavier(ks[4], (D_MODEL, D_MODEL))
        bq = jnp.zeros((D_MODEL,), jnp.float32)
        bk = jnp.zeros((D_MODEL,), jnp.float32)
        bv = jnp.zeros((D_MODEL,), jnp.float32)
        bo = jnp.zeros((D_MODEL,), jnp.float32)
        return {'x': x, 'Wq': Wq, 'bq': bq, 'Wk': Wk, 'bk': bk, 'Wv': Wv, 'bv': bv, 'Wo': Wo, 'bo': bo}
    _L0_attn_in = _L0_attn_setup()

    def _L0_ffn_setup():
        import jax, jax.numpy as jnp
        import numpy as np
        B, S, H, I, E = (2, 512, 128, 64, 8)
        key = jax.random.key(seed)
        ks = jax.random.split(key, 5)
        scale_h = 1.0 / np.sqrt(H)
        scale_i = 1.0 / np.sqrt(I)
        return {'hidden_states': jax.random.normal(ks[0], (B, S, H), dtype=jnp.float32), 'gate_w': jax.random.normal(ks[1], (E, H), dtype=jnp.float32) * scale_h, 'w_gate': jax.random.normal(ks[2], (E, I, H), dtype=jnp.float32) * scale_h, 'w_up': jax.random.normal(ks[3], (E, I, H), dtype=jnp.float32) * scale_h, 'w_down': jax.random.normal(ks[4], (E, H, I), dtype=jnp.float32) * scale_i}
    _L0_ffn_in = _L0_ffn_setup()
    _d = {'L0_attn_x': _L0_attn_in['x'], 'L0_attn_Wq': _L0_attn_in['Wq'], 'L0_attn_bq': _L0_attn_in['bq'], 'L0_attn_Wk': _L0_attn_in['Wk'], 'L0_attn_bk': _L0_attn_in['bk'], 'L0_attn_Wv': _L0_attn_in['Wv'], 'L0_attn_bv': _L0_attn_in['bv'], 'L0_attn_Wo': _L0_attn_in['Wo'], 'L0_attn_bo': _L0_attn_in['bo'], 'L0_ffn_gate_w': _L0_ffn_in['gate_w'], 'L0_ffn_w_gate': _L0_ffn_in['w_gate'], 'L0_ffn_w_up': _L0_ffn_in['w_up'], 'L0_ffn_w_down': _L0_ffn_in['w_down']}
    _x0 = _d['L0_attn_x']
    _d['L0_attn_x'] = jax.random.normal(jax.random.fold_in(jax.random.key(seed), 1), (4, 1024, 128), dtype=_x0.dtype)
    del _x0
    return _d

def reference(L0_attn_x, L0_attn_Wq, L0_attn_bq, L0_attn_Wk, L0_attn_bk, L0_attn_Wv, L0_attn_bv, L0_attn_Wo, L0_attn_bo, L0_ffn_gate_w, L0_ffn_w_gate, L0_ffn_w_up, L0_ffn_w_down):

    def _L0_attn_ref(x, Wq, bq, Wk, bk, Wv, bv, Wo, bo):
        import jax, jax.numpy as jnp
        import numpy as np
        B, S, IN_DIM, D_MODEL, NUM_HEADS = (4, 256, 128, 128, 16)
        HEAD_DIM = D_MODEL // NUM_HEADS
        CAUSAL = True
        NEG = -9000000000000000.0

        def _xavier(key, shape):
            fan_out, fan_in = shape
            limit = (6.0 / (fan_in + fan_out)) ** 0.5
            return jax.random.uniform(key, shape, jnp.float32, -limit, limit)
        batch, seq, _ = x.shape
        q = x @ Wq.T + bq
        k = x @ Wk.T + bk
        v = x @ Wv.T + bv

        def split(t):
            return t.reshape(batch, seq, NUM_HEADS, HEAD_DIM).transpose(0, 2, 1, 3)
        q, k, v = (split(q), split(k), split(v))
        scores = jnp.einsum('bhqd,bhkd->bhqk', q, k) / jnp.sqrt(jnp.float32(HEAD_DIM))
        if CAUSAL:
            mask = jnp.tril(jnp.ones((seq, seq), bool))
            scores = jnp.where(mask, scores, jnp.float32(NEG))
        attn = jax.nn.softmax(scores, axis=-1)
        out = jnp.einsum('bhqk,bhkd->bhqd', attn, v)
        out = out.transpose(0, 2, 1, 3).reshape(batch, seq, D_MODEL)
        return out @ Wo.T + bo

    def _L0_ffn_ref(hidden_states, gate_w, w_gate, w_up, w_down):
        import jax, jax.numpy as jnp
        import numpy as np
        B, S, H, I, E = (2, 512, 128, 64, 8)
        b, s, h = hidden_states.shape
        x = hidden_states.reshape(-1, h)
        logits = x @ gate_w.T
        top_v = jnp.max(logits, axis=-1)
        sel = jnp.argmax(logits, axis=-1)
        rw = jax.nn.sigmoid(top_v)
        out = jnp.zeros_like(x)
        n_exp = gate_w.shape[0]
        for e in range(n_exp):
            mask = (sel == e).astype(x.dtype)
            xs = x * (rw * mask)[:, None]
            g = xs @ w_gate[e].T
            u = xs @ w_up[e].T
            out = out + u * jax.nn.silu(g) @ w_down[e].T
        return out.reshape(b, s, h)
    x = L0_attn_x
    x = x + _L0_attn_ref(_layernorm(x, axis=-1), L0_attn_Wq, L0_attn_bq, L0_attn_Wk, L0_attn_bk, L0_attn_Wv, L0_attn_bv, L0_attn_Wo, L0_attn_bo)
    x = x + _L0_ffn_ref(_layernorm(x, axis=-1), L0_ffn_gate_w, L0_ffn_w_gate, L0_ffn_w_up, L0_ffn_w_down)
    return x

_drawn_inputs = setup_inputs


def setup_inputs(seed=0):
    import zlib

    import numpy as np

    out = dict(_drawn_inputs(seed))
    spreads = {'L0_attn_bq': (0.0, 0.1),
     'L0_attn_bk': (0.0, 0.1),
     'L0_attn_bv': (0.0, 0.1),
     'L0_attn_bo': (0.0, 0.1)}
    factors = {}
    for name, (base, spread) in spreads.items():
        noise = np.random.default_rng([zlib.crc32(name.encode()), seed]).standard_normal(out[name].shape)
        drawn = base * np.exp(spread * noise) if base else spread * noise
        out[name] = jnp.asarray(drawn.astype(out[name].dtype))
    for name, factor in factors.items():
        out[name] = (out[name] * factor).astype(out[name].dtype)
    return out
```

```python
import concourse.bass as bass
from concourse import mybir
from contextlib import ExitStack

FP32 = mybir.dt.float32
BF16 = mybir.dt.bfloat16
ALU = mybir.AluOpType
ACT = mybir.ActivationFunctionType
AX = mybir.AxisListType

P = 128
BATCH, SEQ, DIM = 4, 1024, 128
HEADS, HD = 16, 8
EXPERTS, INNER = 8, 64
PAIRS = EXPERTS // 2
HALF = 512
TPH = HALF // P
TILES = BATCH * SEQ // P
STEPS = BATCH * SEQ // HALF
GH = 4
UNITS = BATCH * HEADS // GH
PARTS_Q = (0, 0, 1, 1, 0, 2)
PARTS_K = (0, 1, 0, 1, 2, 0)
ROWS = len(PARTS_Q) * HD
ROWS_M = ROWS + 3
EPS = 1e-5
SCALE = float(HD) ** -0.5
MASKED = -1e30

SLOTS = [(c, j, max(0, P * j - HALF * c), HALF - max(0, P * j - HALF * c))
         for c in range(2) for j in range(TPH * (c + 1))]
DIAG = [i for i, (c, j, _, _) in enumerate(SLOTS) if j >= TPH * c]
LAST = {c: max(i for i, s in enumerate(SLOTS) if s[0] == c) for c in range(2)}
PIECES = []
for _qt in range(SEQ // P):
    for _g in range(GH):
        if _qt >= TPH:
            PIECES.append((_qt, _g, 0, HALF, False))
        PIECES.append((_qt, _g, HALF * (_qt // TPH), P * (_qt % TPH + 1), True))
ENDS = {c: max(i for i, s in enumerate(PIECES) if s[0] < TPH * (c + 1)) for c in range(2)}
ROT = len(PIECES) + 2
FIRST = len(PIECES) + 1


def unit_order(rows, columns):
    if not columns:
        out = [("piece", n) for n in range(len(PIECES))]
        out.insert(ENDS[0] + 9, ("turn", 0, 1))
        return out
    out, done, n = [], 0, 0
    whole = sum(s[3] for s in PIECES)
    cols = 0
    for i, slot in enumerate(SLOTS):
        for pair in range(2):
            out.append(("scores", i, pair))
            cols += 2 * slot[3]
            while rows and n < len(PIECES) and done < min(whole, 1.08 * cols):
                out.append(("piece", n))
                done += PIECES[n][3]
                n += 1
                if n == ENDS[0] + 9:
                    out.append(("turn", 0, 1))
        if i == 0:
            out.append(("turn", 1, 0))
        else:
            out.append(("values", i - 1))
    out.append(("values", len(SLOTS) - 1))
    return out


def uses(order):
    return [e for e in order if e[0] in ("piece", "turn")]


def layer_kernel(nc, x, wq_t, wk_t, wv_t, wo_t, bq, bk, bv, bo, gate_t, wg_t, wu_t, wd_t, out):
    split = nc.dram_tensor("split_rows", (2, UNITS * GH, ROWS_M, SEQ), BF16, kind="Internal").ap()
    sums = nc.dram_tensor("value_sums", (UNITS, GH, HD + 1, SEQ), FP32, kind="Internal").ap()
    x_tiles = x.rearrange("b (n p) f -> p (b n) f", p=P)
    out_tiles = out.rearrange("b (n p) f -> p (b n) f", p=P)

    ctx = ExitStack()
    with ctx:
        def sb(name, shape, dt=FP32):
            return ctx.enter_context(nc.sbuf_tensor(name, shape, dt))

        def sem(name):
            return ctx.enter_context(nc.semaphore(name))

        w_qkv = sb("w_qkv", [P, 3, DIM])
        w_o = sb("w_o", [P, DIM])
        w_gate = sb("w_gate", [P, EXPERTS])
        w_g = sb("w_g", [P, EXPERTS * INNER])
        w_u = sb("w_u", [P, EXPERTS * INNER])
        w_d = sb("w_d", [P, PAIRS, DIM])
        b_qk = sb("b_qk", [P, 2])
        b_v = sb("b_v", [P, HEADS, HD])
        b_o = sb("b_o", [P, DIM])
        ident = sb("ident", [P, P])
        ident_b = sb("ident_b", [P, P], BF16)
        causal = sb("causal", [P, HALF])
        ramp = sb("ramp", [P, TPH, EXPERTS])
        minus_half = sb("minus_half", [P, TPH])
        x_sb = sb("x_sb", [P, TILES, DIM])
        v_sb = sb("v_sb", [P, UNITS, SEQ // P, GH, HD])
        stats = sb("stats", [P, 2, TPH, 6])
        moments = sb("moments", [P, 2, TPH, 2])
        spread = sb("spread", [P, 2, TPH])
        rstd = sb("rstd", [P, 2, TPH])
        xn = sb("xn", [P, 2, TPH, DIM])
        xn_t = sb("xn_t", [P, 2, HALF])
        qk = sb("qk", [P, 2, 2, HALF])
        rest = sb("rest", [P, 2, 2, HALF])
        part = sb("part", [P, 2, 3, 2, HALF], BF16)
        q_rows = sb("q_rows", [P, 3, GH, SEQ], BF16)
        k_rows = sb("k_rows", [P, 3, GH, SEQ], BF16)
        v_unit = sb("v_unit", [P, 3, SEQ // P, GH, 32])
        prob = sb("prob", [P, 3, GH, HALF])
        junk = sb("junk", [P, 3, HALF], BF16)
        top_a = sb("top_a", [P, SEQ // P, GH])
        top_b = sb("top_b", [P, TPH, GH])
        top = sb("top", [P, TPH, GH])
        top_rest = sb("top_rest", [P, 2, TPH, GH])
        top_part = sb("top_part", [P, 2, TPH, 3, GH], BF16)
        top_rows = sb("top_rows", [12, 2, HALF], BF16)
        sum_sb = sb("sum_sb", [P, 2, HALF])
        numer, denom = qk[:, 0, :, :], qk[:, 1, :, :]
        attn, gated = rest[:, 0, :, :], rest[:, 1, :, :]
        x1 = sb("x1", [P, 2, TPH, DIM])
        best = sb("best", [P, 2, TPH])
        hit = sb("hit", [P, 2, TPH, EXPERTS])
        first = sb("first", [P, 2, TPH])
        chosen = sb("chosen", [P, 2, TPH, EXPERTS], BF16)
        picked = sb("picked", [P, 2, TPH, EXPERTS * INNER], BF16)
        weight = sb("weight", [P, 2, TPH])
        xs = sb("xs", [P, 2, TPH, DIM])
        xs_t = sb("xs_t", [P, 2, HALF])
        hidden, silu = prob[:, 0, :, :], prob[:, 1, 0:2, :]
        y = sb("y", [P, 2, TPH, DIM])
        ps = ctx.enter_context(nc.psum_tensor("ps", [P, 8, HALF], FP32))
        BANK_V = 4

        weights_in = sem("weights_in")
        x_in = sem("x_in")
        zeros_out = sem("zeros_out")
        const_set = sem("const_set")
        v_ones_set = sem("v_ones_set")
        held = sem("held")
        def pair_of(name):
            return [sem(name + "_0"), sem(name + "_1")]
        moments_set = pair_of("moments_set")
        rstd_set = pair_of("rstd_set")
        xn_set = pair_of("xn_set")
        turned = pair_of("turned")
        xn_t_set = pair_of("xn_t_set")
        qk_mm = pair_of("qk_mm")
        v_mm = pair_of("v_mm")
        qk_set = pair_of("qk_set")
        part1_set = pair_of("part1_set")
        rest_set = pair_of("rest_set")
        part2_set = pair_of("part2_set")
        part3_set = pair_of("part3_set")
        v_set = pair_of("v_set")
        split_out = pair_of("split_out")
        dve_chain = sem("dve_chain")
        pool_chain = sem("pool_chain")
        rows_in = [sem(f"rows_in_{k}") for k in range(3)]
        top_in = [[sem(f"top_in_{k}_{c}") for c in range(2)] for k in range(3)]
        scores_mm = sem("scores_mm")
        exp_done = sem("exp_done")
        diag_done = sem("diag_done")
        values_mm = sem("values_mm")
        sum_set = sem("sum_set")
        sum_out = pair_of("sum_out")
        rot_mm = sem("rot_mm")
        rot_free = sem("rot_free")
        top_set = sem("top_set")
        top_part_set = sem("top_part_set")
        v_unit_set = sem("v_unit_set")
        bo_added = sem("bo_added")
        attn_in = pair_of("attn_in")
        inv_set = sem("inv_set")
        attn_set = sem("attn_set")
        proj_mm = sem("proj_mm")
        moments3 = sem("moments3")
        rstd3 = sem("rstd3")
        xn3 = sem("xn3")
        xn_turned = sem("xn_turned")
        xn_t3 = sem("xn_t3")
        logit_mm = sem("logit_mm")
        best_set = sem("best_set")
        tanh_set = sem("tanh_set")
        chosen_set = sem("chosen_set")
        picked_set = sem("picked_set")
        xs_set = sem("xs_set")
        xs_turned = sem("xs_turned")
        xs_t_set = sem("xs_t_set")
        gate_mm = sem("gate_mm")
        up_mm = sem("up_mm")
        pick_mm = sem("pick_mm")
        silu_set = sem("silu_set")
        hidden_set = sem("hidden_set")
        gated_set = sem("gated_set")
        down_mm = sem("down_mm")
        y_set = sem("y_set")
        y_out = pair_of("y_out")

        def hold(eng, s, value):
            eng.wait_ge(s, value)
            if not isinstance(value, int):
                eng.sem_inc(held, 1)

        class Chain:
            def __init__(self, eng, s):
                self.eng, self.s, self.base, self.n = eng, s, 0, 0

            def link(self, ins):
                self.n += 1
                ins.then_inc(self.s, 1)
                hold(self.eng, self.s, self.base + self.n)

        def looped(eng, count, body, per_iteration, chain=None):
            start = chain.n if chain else 0
            with eng.Fori(0, count) as i:
                if chain:
                    chain.base, chain.n = i * per_iteration, start
                body(i)
                if chain:
                    assert chain.n == start + per_iteration, (chain.n, start)
            if chain:
                chain.base, chain.n = 0, start + count * per_iteration

        LOOPS = (UNITS - 1) // 3
        FULL = unit_order(True, True)
        LEAD = unit_order(True, False)
        TAIL = unit_order(False, True)
        assert len(uses(FULL)) == ROT and len(uses(LEAD)) == FIRST

        def at(per, t, k, more=0):
            return t * (3 * per) + (per * k + more)

        def rot(t, k, r):
            return at(ROT, t, k, FIRST + r)

        def rot_before(r):
            return r - 3 if r >= 3 else (-2, -1, -3)[r]

        block = ctx.enter_context(nc.Block())

        @block.sync
        def _(sp):
            for s in split_out + sum_out + y_out + [s for k in top_in for s in k]:
                sp.sem_inc(s, 16)
            sp.dma_start(x_sb[:, 0:TPH, :], x_tiles[:, 0:TPH, :]).then_inc(x_in, 16)
            for dst, src in ((w_qkv[:, 0, :], wq_t), (w_qkv[:, 1, :], wk_t), (w_qkv[:, 2, :], wv_t),
                             (b_qk[:, 0:1], bq), (b_qk[:, 1:2], bk),
                             (b_v[:, :, :], bv.to_broadcast((P, DIM))), (b_o[:], bo.to_broadcast((P, DIM))),
                             (w_o[:], wo_t), (w_gate[:], gate_t), (w_g[:], wg_t), (w_u[:], wu_t),
                             (w_d[:], wd_t.rearrange("(q r) f -> r q f", q=PAIRS))):
                sp.dma_start(dst, src).then_inc(weights_in, 16)
            with sp.Fori(1, STEPS) as n:
                sp.wait_ge(x_in, n * 16)
                sp.dma_start(x_sb[:, bass.ds(n * TPH, TPH), :],
                             x_tiles[:, bass.ds(n * TPH, TPH), :]).then_inc(x_in, 16)

            def write_split(b):
                for h in range(2):
                    for side, parts in ((0, PARTS_Q), (1, PARTS_K)):
                        for r, n in enumerate(parts):
                            if side == 0 and r == 0:
                                sp.wait_ge(part3_set[h], b + 2)
                            sp.dma_start(split[side, bass.ds(b * HEADS, HEADS), r * HD:(r + 1) * HD,
                                               h * HALF:(h + 1) * HALF],
                                         part[:, h, n, side, :]).then_inc(split_out[h], 16)
            with sp.Fori(0, BATCH) as b:
                write_split(b)
            sp.wait_ge(const_set, 6)
            sp.dma_start(split[0, :, ROWS:ROWS_M, :], q_rows[0:UNITS * GH, 0, 0:3, :]).then_inc(zeros_out, 16)
            sp.wait_ge(zeros_out, 16)
            for h in range(2):
                sp.wait_ge(split_out[h], 16 * 12 * BATCH + 16)


            def load_rows(u, k):
                for side, rows, n in ((0, q_rows, ROWS_M), (1, k_rows, ROWS)):
                    sp.dma_start(rows[0:n, k, :, :], split[side, bass.ds(u * GH, GH), 0:n, :]
                                 .rearrange("g r t -> r g t")).then_inc(rows_in[k], 16)

            def send_top(t, k, c):
                sp.dma_start(q_rows[ROWS:ROWS_M, k, :, c * HALF:(c + 1) * HALF],
                             top_rows[:, c, :]).then_inc(top_in[k][c], 16)

            def send_sums(t, k, c):
                sp.wait_ge(sum_set, at(2, t, k, c + 2))
                for g in range(GH):
                    sp.dma_start(sums[bass.ds(at(1, t, k), 1), g, :, c * HALF:(c + 1) * HALF],
                                 sum_sb[32 * g:32 * g + HD + 1, c, :]).then_inc(sum_out[c], 16)

            def turn_use(order, c, nxt):
                return [n for n, e in enumerate(uses(order)) if e == ("turn", c, nxt)][0]

            load_rows(0, 0)
            load_rows(1, 1)
            sp.wait_ge(rot_free, turn_use(LEAD, 0, 1) + 1)
            send_top(0, 0, 0)

            def step(t, k, load, rows):
                nt, nk = (t, k + 1) if k < 2 else (t + 1, 0)
                lt, lk = (t, k + 2) if k < 1 else (t + 1, k - 1)
                if load:
                    sp.wait_ge(scores_mm, at(24, t, k, 1))
                    load_rows(at(1, lt, lk), lk)
                order = FULL if rows else TAIL
                sp.wait_ge(rot_free, rot(t, k, turn_use(order, 1, 0) + 1))
                send_top(t, k, 1)
                if rows:
                    sp.wait_ge(rot_free, rot(t, k, turn_use(order, 0, 1) + 1))
                    send_top(nt, nk, 0)
                send_sums(t, k, 0)
                send_sums(t, k, 1)

            with sp.Fori(0, LOOPS - 1) as t:
                for k in range(3):
                    step(t, k, True, True)
            for k in range(3):
                step(LOOPS - 1, k, k < 2, True)
            step(LOOPS, 0, False, False)
            for c in range(2):
                sp.wait_ge(sum_out[c], 64 * UNITS + 16)

            def load_attn(b, h):
                sp.dma_start(numer[:, h, :], sums[bass.ds(b * GH, GH), :, 0:HD, h * HALF:(h + 1) * HALF]
                             .rearrange("u g d t -> (u g) d t")).then_inc(attn_in[h], 16)
                sp.dma_start(denom[:, h, :], sums[bass.ds(b * GH, GH), :, HD:HD + 1, h * HALF:(h + 1) * HALF]
                             .rearrange("u g d t -> (u g) d t").to_broadcast((HEADS, HD, HALF))
                             ).then_inc(attn_in[h], 16)

            def store(t, h):
                sp.wait_ge(y_set, t * 2 + (h + 2))
                sp.dma_start(out_tiles[:, bass.ds(t * (2 * TPH) + h * TPH, TPH), :],
                             y[:, h, :, :]).then_inc(y_out[h], 16)

            load_attn(0, 0)
            load_attn(0, 1)
            with sp.Fori(0, BATCH - 1) as t:
                for h in range(2):
                    sp.wait_ge(attn_set, t * 2 + (h + 1))
                    load_attn(t + 1, h)
                    store(t, h)
            for h in range(2):
                store(BATCH - 1, h)
            for h in range(2):
                sp.wait_ge(y_out[h], 16 * BATCH + 16)

        @block.gpsimd
        def _(pool):
            chain = Chain(pool, pool_chain)
            g = nc.gpsimd
            for s in part3_set:
                pool.sem_inc(s, 1)
            chain.link(g.memset(ident[:], 0.0))
            chain.link(g.affine_select(out=ident[:], in_=ident[:], pattern=[[-1, P]], base=0,
                                       channel_multiplier=1, compare_op=ALU.not_equal, fill=1.0))
            g.tensor_copy(ident_b[:], ident[:]).then_inc(const_set, 1)
            g.memset(minus_half[:], -0.5).then_inc(const_set, 1)
            chain.link(g.memset(causal[:], 0.0))
            g.affine_select(out=causal[:, HALF - P:], in_=causal[:, HALF - P:], pattern=[[-1, P]], base=0,
                            channel_multiplier=1, compare_op=ALU.is_ge, fill=MASKED).then_inc(const_set, 1)
            for e in range(EXPERTS):
                last = g.memset(ramp[:, :, e:e + 1], float(EXPERTS - e))
            last.then_inc(const_set, 1)

            def rsqrt(h, dst_sem):
                chain.link(g.tensor_scalar(spread[:, h, :], moments[:, h, :, 1], EPS, None, ALU.add))
                g.tensor_tensor(rstd[:, h, :], spread[:, h, :], minus_half[:], ALU.pow).then_inc(dst_sem, 1)

            g.memset(q_rows[:], 0.0).then_inc(const_set, 1)
            g.memset(k_rows[:], -1.0).then_inc(const_set, 1)
            chain.link(g.memset(v_unit[:], 0.0))
            g.memset(v_unit[:, :, :, :, HD:HD + 1], 1.0).then_inc(v_ones_set, 1)
            pool.wait_ge(const_set, 4)

            def norm_step(b):
                for h in range(2):
                    hold(pool, moments_set[h], b + 1)
                    rsqrt(h, rstd_set[h])
                    if h == 1:
                        third(b, 0)
                third(b, 1)

            def third(b, h):
                hold(pool, part2_set[h], b + 1)
                g.tensor_tensor(part[:, h, 2, :, :], rest[:, h, :, :], part[:, h, 1, :, :],
                                ALU.subtract).then_inc(part3_set[h], 1)
            looped(pool, BATCH, norm_step, 2, chain)

            pool.wait_ge(weights_in, 16 * 12)
            for h in range(2):
                pool.wait_ge(v_set[h], BATCH + 1)

            def copy_v(u, k):
                g.tensor_copy(v_unit[:, k, :, :, 0:HD], v_sb[:, bass.ds(u, 1), :, :, :]
                              .rearrange("p u j g d -> p (u j) g d")).then_inc(v_unit_set, 1)

            pool.wait_ge(v_ones_set, 1)
            copy_v(0, 0)

            def split_top(c):
                src = top_a[:, 0:TPH, :] if c == 0 else top[:]
                chain.link(g.tensor_copy(top_part[:, c, :, 0, :], src))
                chain.link(g.tensor_tensor(top_rest[:, c], src, top_part[:, c, :, 0, :], ALU.subtract))
                chain.link(g.tensor_copy(top_part[:, c, :, 1, :], top_rest[:, c]))
                g.tensor_tensor(top_part[:, c, :, 2, :], top_rest[:, c], top_part[:, c, :, 1, :],
                                ALU.subtract).then_inc(top_part_set, 1)

            pool.wait_ge(rot_free, 16)
            split_top(0)
            pool.wait_ge(top_set, 1)
            split_top(1)

            def step(t, k, rows):
                nt, nk = (t, k + 1) if k < 2 else (t + 1, 0)
                order = FULL if rows else TAIL
                r, d = 0, 0
                for e in order:
                    if e[0] in ("piece", "turn"):
                        r += 1
                    if e == ("piece", ENDS[0] + 2):
                        hold(pool, rot_free, rot(t, k, r - 2))
                        split_top(0)
                    if e[0] == "scores" and e[1] in DIAG:
                        i, p = e[1], e[2]
                        hold(pool, exp_done, at(24, t, k, 2 + 2 * i + p + 1))
                        blockv = prob[:, i % 3, 2 * p:2 * p + 2, 0:P]
                        g.affine_select(out=blockv, in_=blockv, pattern=[[0, 2], [1, P]], base=0,
                                        channel_multiplier=-1, compare_op=ALU.is_ge,
                                        fill=0.0).then_inc(diag_done, 1)
                        if rows and i == 8 and p == 0:
                            hold(pool, values_mm, at(12, t, k, 3 + 1))
                            copy_v(at(1, nt, nk), nk)
                if rows:
                    hold(pool, top_set, at(1, t, k, 2))
                    split_top(1)

            def three(t):
                for k in range(3):
                    step(t, k, True)
            looped(pool, LOOPS, three, 18, chain)
            step(LOOPS, 0, False)

            def add_bo(i):
                for j in range(TPH):
                    last = g.tensor_tensor(x_sb[:, bass.ds(i * TPH + j, 1), :],
                                           x_sb[:, bass.ds(i * TPH + j, 1), :], b_o[:, None, :], ALU.add)
                last.then_inc(bo_added, 1)
            with pool.Fori(0, STEPS) as i:
                add_bo(i)

            def front(n, h):
                hold(pool, inv_set, n)
                g.tensor_tensor(attn[:, h, :], numer[:, h, :], denom[:, h, :], ALU.mult).then_inc(attn_set, 1)
                hold(pool, moments3, n)
                rsqrt(h, rstd3)
                hold(pool, chosen_set, n)
                g.tensor_copy(picked[:, h].rearrange("p n (e i) -> p (n e) i", e=EXPERTS),
                              chosen[:, h].rearrange("p n e -> p (n e)")[:, :, None]
                              .to_broadcast((P, TPH * EXPERTS, INNER))).then_inc(picked_set, 1)

            front(1, 0)

            def two(t):
                front(t * 2 + 2, 1)
                front(t * 2 + 3, 0)
            looped(pool, BATCH - 1, two, 2, chain)
            front(STEPS, 1)

        @block.scalar
        def _(act):
            a = nc.scalar
            for s in xn_t_set + qk_set + [sum_set]:
                act.sem_inc(s, 1)
            act.wait_ge(weights_in, 16 * 12)
            with act.Fori(0, BATCH) as b:
                for h in range(2):
                    act.wait_ge(turned[h], b + 2)
                    act.wait_ge(v_mm[h], b + 1)
                    a.activation(xn_t[:, h, :], ps[:, 4 * h, :], ACT.Copy).then_inc(xn_t_set[h], 1)
                    act.wait_ge(qk_mm[h], b + 1)
                    act.wait_ge(part3_set[h], b + 1)
                    for side in range(2):
                        last = a.activation(qk[:, h, side, :], ps[:, 4 * h + 1 + side, :], ACT.Identity,
                                            bias=b_qk[:, side:side + 1])
                    last.then_inc(qk_set[h], 1)
                    act.wait_ge(split_out[h], b * (16 * 12) + 16)
                    act.wait_ge(qk_set[h], b + 2)
                    a.activation(part[:, h, 0, :, :], qk[:, h, :, :], ACT.Copy).then_inc(part1_set[h], 1)
                    act.wait_ge(rest_set[h], b + 1)
                    a.activation(part[:, h, 1, :, :], rest[:, h, :, :], ACT.Copy).then_inc(part2_set[h], 1)

            act.sem_inc(exp_done, 2)
            chunk_end = {LAST[0] + 1: 0}

            def take_sums(t, k, c):
                act.wait_ge(values_mm, at(12, t, k, 3 + LAST[c] + 1))
                act.wait_ge(sum_out[c], at(64, t, k, 16))
                a.activation(sum_sb[:, c, :], ps[:, BANK_V, :], ACT.Copy).then_inc(sum_set, 1)

            def step(t, k):
                for i, (c, j, q0, n) in enumerate(SLOTS):
                    for p in range(2):
                        e = 2 * i + p
                        act.wait_ge(scores_mm, at(24, t, k, e + 1))
                        if p == 0:
                            act.wait_ge(values_mm, at(12, t, k, i + 1))
                        a.activation(prob[:, i % 3, 2 * p:2 * p + 2, 0:n],
                                     ps[:, 2 * (e % 2):2 * (e % 2) + 2, 0:n], ACT.Exp,
                                     scale=SCALE).then_inc(exp_done, 1)
                    if i in chunk_end:
                        take_sums(t, k, chunk_end[i])
                take_sums(t, k, 1)

            with act.Fori(0, LOOPS) as t:
                for k in range(3):
                    step(t, k)
            step(LOOPS, 0)

            def front(n, h):
                act.wait_ge(xn_turned, n)
                a.activation(xn_t[:, h, :], ps[:, 1, :], ACT.Copy).then_inc(xn_t3, 1)
                yield
                act.wait_ge(best_set, n)
                a.activation(weight[:, h, :], best[:, h, :], ACT.Tanh, scale=0.5).then_inc(tanh_set, 1)
                yield
                act.wait_ge(xs_turned, n)
                a.activation(xs_t[:, h, :], ps[:, 1, :], ACT.Copy).then_inc(xs_t_set, 1)
                yield

            def back(n, pr):
                act.wait_ge(gate_mm, n + pr + 1)
                act.wait_ge(gated_set, n + (pr + 1))
                a.activation(silu[:, pr % 2, :], ps[:, 2 + pr % 2, :], ACT.Silu).then_inc(silu_set, 1)

            act.sem_inc(silu_set, 2)
            for _ in front(1, 0):
                pass

            def both(done, nxt, h):
                f = front(nxt, h) if nxt is not None else iter(())
                back(done, 0)
                next(f, None)
                back(done, 1)
                back(done, 2)
                next(f, None)
                next(f, None)
                back(done, 3)

            with act.Fori(0, BATCH - 1) as t:
                both(t * 8, t * 2 + 2, 1)
                both(t * 8 + 4, t * 2 + 3, 0)
            both(8 * (BATCH - 1), STEPS, 1)
            both(8 * (BATCH - 1) + 4, None, 0)

        @block.vector
        def _(dve):
            chain = Chain(dve, dve_chain)
            v = nc.vector
            for s in v_set + [y_set, hidden_set]:
                dve.sem_inc(s, 1)
            dve.wait_ge(const_set, 4)
            dve.wait_ge(weights_in, 16 * 12)

            def count_moments(src, h, done):
                for i in range(TPH):
                    last = v.bn_stats(stats[:, h, i, :], src(i))
                chain.link(last)
                for i in range(TPH):
                    last = v.bn_aggr(moments[:, h, i, :], stats[:, h, i, :])
                last.then_inc(done, 1)

            def normalise(src, h, done):
                for i in range(TPH):
                    last = v.tensor_scalar(xn[:, h, i, :], src(i), moments[:, h, i, 0:1], rstd[:, h, i:i + 1],
                                           ALU.subtract, ALU.mult)
                last.then_inc(done, 1)

            def x_of(b, h):
                return lambda i: x_sb[:, bass.ds(b * (2 * TPH) + h * TPH + i, 1), :].rearrange("p n f -> p (n f)")

            def phase1(b):
                for h in range(2):
                    hold(dve, x_in, b * 32 + 16 * (h + 1))
                    count_moments(x_of(b, h), h, moments_set[h])
                    hold(dve, turned[h], b + 1)
                    hold(dve, rstd_set[h], b + 1)
                    normalise(x_of(b, h), h, xn_set[h])
                    if h == 1:
                        split_rest(b, 0)
                split_rest(b, 1)

            def split_rest(b, h):
                hold(dve, part1_set[h], b + 1)
                v.tensor_tensor(rest[:, h, :, :], qk[:, h, :, :], part[:, h, 0, :, :],
                                ALU.subtract).then_inc(rest_set[h], 1)
                hold(dve, v_mm[h], b + 2)
                psum_v = ps[:, 4 * h + 3, :].rearrange("p (j u g d) -> p j u g d", j=TPH, u=GH, g=GH)
                for q in range(GH):
                    last = v.tensor_tensor(
                        v_sb[:, bass.ds(b * GH + q, 1), h * TPH:(h + 1) * TPH, :, :]
                        .rearrange("p u j g d -> p (u j) g d"),
                        psum_v[:, :, q, :, :],
                        b_v[:, None, q * GH:(q + 1) * GH, :].to_broadcast((P, TPH, GH, HD)), ALU.add)
                last.then_inc(v_set[h], 1)
            looped(dve, BATCH, phase1, 2, chain)

            def piece(n, bank):
                qt, head, k0, cols, diag = PIECES[n]
                if diag:
                    return v.tensor_tensor_reduce(
                        out=junk[:, bank, 0:cols], in0=ps[:, 5 + bank, 0:cols], in1=causal[:, HALF - cols:],
                        scale=1.0, scalar=-3e38, op0=ALU.add, op1=ALU.max,
                        accum_out=top_a[:, qt, head:head + 1])
                return v.tensor_reduce(top_b[:, qt - TPH, head:head + 1], ps[:, 5 + bank, 0:cols], AX.X, ALU.max)

            def turn(c, bank):
                src = ps[0:12, 5 + bank, :].bitcast(BF16)[:, 0:HALF]
                return v.tensor_copy(top_rows[:, c, :], src)

            def join(count):
                hold(dve, rot_free, count)
                v.tensor_tensor(top[:], top_a[:, TPH:, :], top_b[:], ALU.max).then_inc(top_set, 1)

            for r, e in enumerate(uses(LEAD)):
                dve.wait_ge(rot_mm, r + 1)
                bank = (r + 1) % 3
                ins = piece(e[1], bank) if e[0] == "piece" else turn(e[1], bank)
                ins.then_inc(rot_free, 1)
            join(FIRST)

            def step(t, k, rows):
                order = uses(FULL if rows else TAIL)
                kb, tb = (k - 1, t) if k else (2, t - 1)
                for r, e in enumerate(order):
                    if e[0] == "turn" and e[1] == 1:
                        hold(dve, top_in[kb][1], (tb + 1) * 16 + 16)
                    if e[0] == "turn" and e[1] == 0:
                        hold(dve, top_in[k][0], t * 16 + 32)
                    hold(dve, rot_mm, rot(t, k, r + 1))
                    ins = piece(e[1], r % 3) if e[0] == "piece" else turn(e[1], r % 3)
                    ins.then_inc(rot_free, 1)
                if rows:
                    join(rot(t, k, len(order)))

            with dve.Fori(0, LOOPS) as t:
                for k in range(3):
                    step(t, k, True)
            step(LOOPS, 0, False)

            def x1_of(h):
                return lambda i: x1[:, h, i, :]

            def front(n, b, h):
                hold(dve, attn_in[h], b * 32 + 32)
                v.reciprocal(denom[:, h, :], denom[:, h, :]).then_inc(inv_set, 1)
                yield
                hold(dve, bo_added, n)
                hold(dve, proj_mm, n)
                chain.link(v.tensor_tensor(x1[:, h, :, :], ps[:, 0, :].rearrange("p (n f) -> p n f", n=TPH),
                                           x_sb[:, bass.ds(b * (2 * TPH) + h * TPH, TPH), :], ALU.add))
                count_moments(x1_of(h), h, moments3)
                hold(dve, rstd3, n)
                normalise(x1_of(h), h, xn3)
                yield
                hold(dve, logit_mm, n)
                logits = ps[:, 0, 0:TPH * EXPERTS].rearrange("p (n e) -> p n e", n=TPH)
                ins = v.tensor_reduce(best[:, h, :], logits, AX.X, ALU.max)
                ins.then_inc(best_set, 1)
                hold(dve, best_set, n)
                chain.link(v.tensor_tensor(hit[:, h], logits,
                                           best[:, h, :, None].to_broadcast((P, TPH, EXPERTS)), ALU.is_equal))
                chain.link(v.tensor_tensor(hit[:, h], hit[:, h], ramp[:], ALU.mult))
                chain.link(v.tensor_reduce(first[:, h, :], hit[:, h], AX.X, ALU.max))
                v.tensor_tensor(chosen[:, h], hit[:, h],
                                first[:, h, :, None].to_broadcast((P, TPH, EXPERTS)),
                                ALU.is_equal).then_inc(chosen_set, 1)
                hold(dve, tanh_set, n)
                chain.link(v.tensor_scalar(weight[:, h, :], weight[:, h, :], 0.5, 0.5, ALU.mult, ALU.add))
                for i in range(TPH):
                    last = v.tensor_scalar(xs[:, h, i, :], xn[:, h, i, :], weight[:, h, i:i + 1], None, ALU.mult)
                last.then_inc(xs_set, 1)
                yield

            def back(n4, pr):
                hold(dve, up_mm, n4 + pr + 1)
                hold(dve, silu_set, n4 + pr + 3)
                v.tensor_tensor(gated[:, pr % 2, :], ps[:, 4 + pr % 2, :], silu[:, pr % 2, :],
                                ALU.mult).then_inc(gated_set, 1)
                hold(dve, gated_set, n4 + (pr + 1) + 2)
                hold(dve, pick_mm, n4 + pr + 1)
                v.tensor_tensor(hidden[:, pr, :], ps[:, 6, :], gated[:, pr % 2, :],
                                ALU.mult).then_inc(hidden_set, 1)

            def finish(n, b, h):
                hold(dve, down_mm, n)
                hold(dve, y_out[h], b * 16 + 16)
                v.tensor_tensor(y[:, h, :, :], ps[:, 7, :].rearrange("p (n f) -> p n f", n=TPH),
                                x1[:, h, :, :], ALU.add).then_inc(y_set, 1)

            dve.sem_inc(gated_set, 2)
            for _ in front(1, 0, 0):
                pass

            def both(n4, n, b, h, nb=None):
                f = front(n + 1, nb, 1 - h) if nb is not None else iter(())
                next(f, None)
                back(n4, 0)
                next(f, None)
                back(n4, 1)
                back(n4, 2)
                next(f, None)
                back(n4, 3)
                finish(n, b, h)

            def two(t):
                both(t * 8, t * 2 + 1, t, 0, t)
                both(t * 8 + 4, t * 2 + 2, t, 1, t + 1)
            looped(dve, BATCH - 1, two, 12, chain)
            last_b = BATCH - 1
            both(last_b * 8, last_b * 2 + 1, last_b, 0, last_b)
            both(last_b * 8 + 4, last_b * 2 + 2, last_b, 1)

        @block.tensor
        def _(pe):
            mm = nc.tensor.matmul
            for s in turned + v_mm:
                pe.sem_inc(s, 1)
            pe.wait_ge(const_set, 4)
            pe.wait_ge(weights_in, 16 * 12)

            def turn_tiles(src, bank):
                for i in range(TPH):
                    last = nc.tensor.transpose(ps[:, bank, i * P:(i + 1) * P], src[:, i, :], ident[:])
                return last

            def turn1(b, h):
                pe.wait_ge(xn_set[h], b + 1)
                pe.wait_ge(xn_t_set[h], b + 1)
                turn_tiles(xn[:, h], 4 * h).then_inc(turned[h], 1)

            def project(b, h):
                pe.wait_ge(xn_t_set[h], b + 2)
                pe.wait_ge(qk_set[h], b + 1)
                for side in range(2):
                    last = mm(ps[:, 4 * h + 1 + side, :], w_qkv[:, side, :], xn_t[:, h, :], start=True, stop=True)
                last.then_inc(qk_mm[h], 1)
                pe.wait_ge(v_set[h], b + 1)
                for i in range(TPH):
                    last = mm(ps[:, 4 * h + 3, i * P:(i + 1) * P], xn_t[:, h, i * P:(i + 1) * P],
                              w_qkv[:, 2, :], start=True, stop=True)
                last.then_inc(v_mm[h], 1)

            with pe.Fori(0, BATCH) as b:
                turn1(b, 0)
                turn1(b, 1)
                project(b, 0)
                project(b, 1)
            for h in range(2):
                pe.wait_ge(qk_set[h], BATCH + 1)
                pe.wait_ge(v_set[h], BATCH + 1)

            def rows_piece(n, k, bank):
                qt, head, k0, cols, _ = PIECES[n]
                return mm(ps[:, 5 + bank, 0:cols], q_rows[:, k, head, qt * P:(qt + 1) * P],
                          k_rows[:, k, head, k0:k0 + cols], start=True, stop=True)

            def turn_top(c, bank):
                bank_b = ps[0:12, 5 + bank, :].bitcast(BF16)
                for i in range(TPH):
                    last = nc.tensor.transpose(bank_b[:, i * P:(i + 1) * P],
                                               top_part[:, c, i].rearrange("p r g -> p (r g)"), ident_b[:])
                return last

            pe.wait_ge(rows_in[0], 32)
            for r, e in enumerate(uses(LEAD)):
                if r >= 3:
                    pe.wait_ge(rot_free, r - 2)
                if e[0] == "turn":
                    pe.wait_ge(top_part_set, 1)
                bank = (r + 1) % 3
                ins = rows_piece(e[1], 0, bank) if e[0] == "piece" else turn_top(0, bank)
                ins.then_inc(rot_mm, 1)

            def step(t, k, rows):
                nt, nk = (t, k + 1) if k < 2 else (t + 1, 0)
                r = 0
                first_piece = True
                for e in (FULL if rows else TAIL):
                    if e[0] == "scores":
                        i, p = e[1], e[2]
                        c, j, q0, n = SLOTS[i]
                        x0 = 2 * i + p
                        if p == 0 and j == 0:
                            pe.wait_ge(top_in[k][c], t * 16 + 32)
                        pe.wait_ge(exp_done, at(24, t, k, x0 + 1))
                        for s in range(2):
                            last = mm(ps[:, 2 * (x0 % 2) + s, 0:n],
                                      k_rows[:, k, 2 * p + s, j * P:(j + 1) * P],
                                      q_rows[:, k, 2 * p + s, c * HALF + q0:(c + 1) * HALF],
                                      start=True, stop=True)
                        last.then_inc(scores_mm, 1)
                    elif e[0] == "values":
                        i = e[1]
                        c, j, q0, n = SLOTS[i]
                        if i == 0:
                            pe.wait_ge(v_unit_set, at(1, t, k, 1))
                        if j == 0:
                            pe.wait_ge(sum_set, at(2, t, k, c + 1))
                        if i in DIAG:
                            pe.wait_ge(diag_done, at(2 * len(DIAG), t, k, 2 * DIAG.index(i) + 2))
                        else:
                            pe.wait_ge(exp_done, at(24, t, k, 2 + 2 * i + 2))
                        for g in range(GH):
                            last = mm(ps[32 * g:32 * g + 32, BANK_V, q0:HALF], v_unit[:, k, j, g, :],
                                      prob[:, i % 3, g, 0:n], start=(j == 0), stop=(i == LAST[c]))
                        last.then_inc(values_mm, 1)
                    else:
                        if e[0] == "piece" and first_piece:
                            pe.wait_ge(rows_in[nk], (nt + 1) * 32)
                            first_piece = False
                        if e[0] == "turn":
                            pe.wait_ge(top_part_set, at(2, t, k, 2 if e[1] else 3))
                        pe.wait_ge(rot_free, rot(t, k, rot_before(r) + 1))
                        ins = rows_piece(e[1], nk, r % 3) if e[0] == "piece" else turn_top(e[1], r % 3)
                        ins.then_inc(rot_mm, 1)
                        r += 1

            pe.sem_inc(values_mm, 3)
            with pe.Fori(0, LOOPS) as t:
                for k in range(3):
                    step(t, k, True)
            step(LOOPS, 0, False)
            pe.wait_ge(sum_set, 2 * UNITS + 1)
            pe.wait_ge(rot_free, FIRST + ROT * (UNITS - 1) + 1)

            def front(n, h):
                pe.wait_ge(attn_set, n)
                for i in range(TPH):
                    last = mm(ps[:, 0, i * P:(i + 1) * P], attn[:, h, i * P:(i + 1) * P], w_o[:],
                              start=True, stop=True)
                last.then_inc(proj_mm, 1)
                yield
                pe.wait_ge(xn3, n)
                turn_tiles(xn[:, h], 1).then_inc(xn_turned, 1)
                yield
                pe.wait_ge(xn_t3, n)
                for i in range(TPH):
                    last = mm(ps[:, 0, i * EXPERTS:(i + 1) * EXPERTS], xn_t[:, h, i * P:(i + 1) * P], w_gate[:],
                              start=True, stop=True)
                last.then_inc(logit_mm, 1)
                yield
                pe.wait_ge(xs_set, n)
                turn_tiles(xs[:, h], 1).then_inc(xs_turned, 1)
                yield

            def back(n, n4, h, pr):
                if pr == 0:
                    pe.wait_ge(xs_t_set, n)
                    pe.wait_ge(picked_set, n)
                cols = slice(pr * P, (pr + 1) * P)
                pe.wait_ge(silu_set, n4 + (pr + 1))
                mm(ps[:, 2 + pr % 2, :], w_g[:, cols], xs_t[:, h, :], start=True, stop=True).then_inc(gate_mm, 1)
                pe.wait_ge(gated_set, n4 + (pr + 1))
                mm(ps[:, 4 + pr % 2, :], w_u[:, cols], xs_t[:, h, :], start=True, stop=True).then_inc(up_mm, 1)
                pe.wait_ge(hidden_set, n4 + (pr + 1))
                for i in range(TPH):
                    last = mm(ps[:, 6, i * P:(i + 1) * P],
                              picked[:, h, i, cols],
                              ident_b[:], start=True, stop=True)
                last.then_inc(pick_mm, 1)

            def down(n, n4):
                pe.wait_ge(hidden_set, n4 + PAIRS + 1)
                pe.wait_ge(y_set, n)
                for i in range(TPH):
                    for pr in range(PAIRS):
                        last = mm(ps[:, 7, i * P:(i + 1) * P], hidden[:, pr, i * P:(i + 1) * P], w_d[:, pr, :],
                                  start=(pr == 0), stop=(pr == PAIRS - 1))
                last.then_inc(down_mm, 1)

            for _ in front(1, 0):
                pass

            def both(n, n4, h, more=True):
                f = front(n + 1, 1 - h) if more else iter(())
                for pr in range(PAIRS):
                    next(f, None)
                    back(n, n4, h, pr)
                down(n, n4)

            with pe.Fori(0, BATCH - 1) as t:
                both(t * 2 + 1, t * 8, 0)
                both(t * 2 + 2, t * 8 + 4, 1)
            last_b = BATCH - 1
            both(last_b * 2 + 1, last_b * 8, 0)
            both(last_b * 2 + 2, last_b * 8 + 4, 1, False)


def kernel(L0_attn_x, L0_attn_Wq, L0_attn_bq, L0_attn_Wk, L0_attn_bk, L0_attn_Wv, L0_attn_bv, L0_attn_Wo,
           L0_attn_bo, L0_ffn_gate_w, L0_ffn_w_gate, L0_ffn_w_up, L0_ffn_w_down):
    import numpy as np
    import concourse.bacc as bacc
    from concourse.bass_utils import run_bass_kernel_spmd

    def t(w):
        return np.ascontiguousarray(np.asarray(w).T)

    rows = EXPERTS * INNER
    given = {
        "x": np.asarray(L0_attn_x),
        "wq_t": t(L0_attn_Wq), "wk_t": t(L0_attn_Wk), "wv_t": t(L0_attn_Wv), "wo_t": t(L0_attn_Wo),
        "bq": np.asarray(L0_attn_bq).reshape(DIM, 1), "bk": np.asarray(L0_attn_bk).reshape(DIM, 1),
        "bv": np.asarray(L0_attn_bv).reshape(1, DIM), "bo": np.asarray(L0_attn_bo).reshape(1, DIM),
        "gate_t": t(L0_ffn_gate_w),
        "wg_t": t(np.asarray(L0_ffn_w_gate).reshape(rows, DIM)),
        "wu_t": t(np.asarray(L0_ffn_w_up).reshape(rows, DIM)),
        "wd_t": np.ascontiguousarray(np.asarray(L0_ffn_w_down).transpose(0, 2, 1)).reshape(rows, DIM),
    }
    nc = bacc.Bacc("TRN2", target_bir_lowering=False, num_devices=1)
    args = [nc.dram_tensor(n, a.shape, FP32, kind="ExternalInput").ap() for n, a in given.items()]
    out = nc.dram_tensor("out", (BATCH, SEQ, DIM), FP32, kind="ExternalOutput").ap()
    layer_kernel(nc, *args, out)
    r = run_bass_kernel_spmd(nc, [given], core_ids=[0])
    return r.results[0]["out"]
```

```python
import concourse.bass as bass
from concourse import mybir
from contextlib import ExitStack

FP32 = mybir.dt.float32
BF16 = mybir.dt.bfloat16
ALU = mybir.AluOpType
ACT = mybir.ActivationFunctionType
AX = mybir.AxisListType

P = 128
BATCH, SEQ, DIM = 4, 1024, 128
HEADS, HD = 16, 8
EXPERTS, INNER = 8, 64
PAIRS = EXPERTS // 2
HALF = 512
TPH = HALF // P
TILES = BATCH * SEQ // P
STEPS = BATCH * SEQ // HALF
GH = 4
UNITS = BATCH * HEADS // GH
PART_ROWS = ((0, 3), (3, 2), (5, 1))
ROWS = 6 * HD
ROWS_M = ROWS + 3
EPS = 1e-5
SCALE = float(HD) ** -0.5
MASKED = -1e30

SLOTS = [(c, j, max(0, P * j - HALF * c), HALF - max(0, P * j - HALF * c))
         for c in range(2) for j in range(TPH * (c + 1))]
DIAG = [i for i, (c, j, _, _) in enumerate(SLOTS) if j >= TPH * c]
LAST = {c: max(i for i, s in enumerate(SLOTS) if s[0] == c) for c in range(2)}
PIECES = []
for _qt in range(SEQ // P):
    for _g in range(GH):
        if _qt >= TPH:
            PIECES.append((_qt, _g, 0, HALF, False))
        PIECES.append((_qt, _g, HALF * (_qt // TPH), P * (_qt % TPH + 1), True))
ENDS = {c: max(i for i, s in enumerate(PIECES) if s[0] < TPH * (c + 1)) for c in range(2)}
ROT = len(PIECES) + 2
FIRST = len(PIECES) + 1


MERGED = ("SPPSPPPPPSaPSPPSPVPPSPSVPSPPSPVPSVPPSPPSPPV"
          "PPPSPSPVPSPPVPSbPPSPSPVPPSPSPVSPSPPSVSPPVPV")


def unit_order(rows, columns):
    if not columns:
        out = [("piece", n) for n in range(len(PIECES))]
        out.insert(ENDS[0] + 9, ("turn", 0, 1))
        return out
    seen = {"S": 0, "V": 0, "P": 0}
    out = []
    for letter in MERGED:
        n = seen.get(letter, 0)
        seen[letter] = n + 1
        if letter == "S":
            out.append(("scores", n // 2, n % 2))
        elif letter == "V":
            out.append(("values", n))
        elif letter == "a":
            out.append(("turn", 1, 0))
        elif rows:
            out.append(("piece", n) if letter == "P" else ("turn", 0, 1))
    assert seen["S"] == 2 * len(SLOTS) and seen["V"] == len(SLOTS) and seen["P"] == len(PIECES)
    return out


def uses(order):
    return [e for e in order if e[0] in ("piece", "turn")]


def layer_kernel(nc, x, wq_t, wk_t, wv_t, wo_t, bq, bk, bv, bo, gate_t, wg_t, wu_t, wd_t, out):
    split = nc.dram_tensor("split_parts", (2, 3, UNITS, HD, GH * SEQ), BF16, kind="Internal").ap()
    inverse = nc.dram_tensor("inverse_sums", (UNITS * GH, SEQ), FP32, kind="Internal").ap()
    sums = nc.dram_tensor("value_sums", (UNITS, GH, HD + 1, SEQ), FP32, kind="Internal").ap()
    x_tiles = x.rearrange("b (n p) f -> p (b n) f", p=P)
    out_tiles = out.rearrange("b (n p) f -> p (b n) f", p=P)

    ctx = ExitStack()
    with ctx:
        def sb(name, shape, dt=FP32):
            return ctx.enter_context(nc.sbuf_tensor(name, shape, dt))

        def sem(name):
            return ctx.enter_context(nc.semaphore(name))

        w_qkv = sb("w_qkv", [P, 3, DIM])
        w_o = sb("w_o", [P, DIM])
        w_gate = sb("w_gate", [P, EXPERTS])
        w_g = sb("w_g", [P, EXPERTS * INNER])
        w_u = sb("w_u", [P, EXPERTS * INNER])
        w_d = sb("w_d", [P, PAIRS, DIM])
        b_qk = sb("b_qk", [P, 2])
        b_v = sb("b_v", [P, 1])
        b_o = sb("b_o", [P, DIM])
        ident = sb("ident", [P, P])
        ident_b = sb("ident_b", [P, P], BF16)
        causal = sb("causal", [P, HALF])
        ramp = sb("ramp", [P, TPH, EXPERTS])
        minus_half = sb("minus_half", [P, TPH])
        x_sb = sb("x_sb", [P, TILES, DIM])
        v_sb = sb("v_sb", [P, UNITS, SEQ // P, GH, HD])
        stats = sb("stats", [P, 2, TPH, 6])
        moments = sb("moments", [P, 2, TPH, 2])
        spread = sb("spread", [P, 2, TPH])
        rstd = sb("rstd", [P, 2, TPH])
        xn = sb("xn", [P, 2, TPH, DIM])
        xn_t = sb("xn_t", [P, 2, HALF])
        qk = sb("qk", [P, 2, 2, HALF])
        rest = sb("rest", [P, 2, 2, HALF])
        part = sb("part", [P, 2, 2, 3, HALF], BF16)
        q_rows = sb("q_rows", [P, 3, GH, SEQ], BF16)
        k_rows = sb("k_rows", [P, 3, GH, SEQ], BF16)
        v_unit = sb("v_unit", [P, 3, SEQ // P, GH, 32])
        prob = sb("prob", [P, 3, GH, HALF])
        junk = sb("junk", [P, 3, HALF], BF16)
        top_a = sb("top_a", [P, SEQ // P, GH])
        top_b = sb("top_b", [P, TPH, GH])
        top = sb("top", [P, TPH, GH])
        top_rest = sb("top_rest", [P, 2, TPH, GH])
        top_part = sb("top_part", [P, 2, TPH, 3, GH], BF16)
        top_rows = sb("top_rows", [12, 2, HALF], BF16)
        sum_sb = sb("sum_sb", [P, 2, HALF])
        numer, denom = qk[:, 0, :, :], qk[:, 1, :, :]
        attn, gated = rest[:, 0, :, :], rest[:, 1, :, :]
        sums_all = prob[:, 2, 0, :]
        best = sb("best", [P, 2, TPH])
        hit = sb("hit", [P, 2, TPH, EXPERTS])
        first = sb("first", [P, 2, TPH])
        chosen = sb("chosen", [P, 2, TPH, EXPERTS], BF16)
        picked = sb("picked", [P, 2, TPH, EXPERTS * INNER], BF16)
        weight = sb("weight", [P, 2, TPH])
        xs = sb("xs", [P, 2, TPH, DIM])
        xs_t = sb("xs_t", [P, 2, HALF])
        hidden, silu = prob[:, 0, :, :], prob[:, 1, 0:2, :]
        y = sb("y", [P, 2, TPH, DIM])
        ps = ctx.enter_context(nc.psum_tensor("ps", [P, 8, HALF], FP32))
        BANK_V = 4

        weights_in = sem("weights_in")
        qkv_in = sem("qkv_in")
        x_in = sem("x_in")
        q_rows_set = sem("q_rows_set")
        k_rows_set = sem("k_rows_set")
        const_set = sem("const_set")
        v_ones_set = sem("v_ones_set")
        held = sem("held")
        def pair_of(name):
            return [sem(name + "_0"), sem(name + "_1")]
        moments_set = pair_of("moments_set")
        rstd_set = pair_of("rstd_set")
        xn_set = pair_of("xn_set")
        turned = pair_of("turned")
        xn_t_set = pair_of("xn_t_set")
        qk_mm = pair_of("qk_mm")
        v_mm = pair_of("v_mm")
        qk_set = pair_of("qk_set")
        part2_set = pair_of("part2_set")
        part3_set = pair_of("part3_set")
        v_set = pair_of("v_set")
        split_out = pair_of("split_out")
        dve_chain = sem("dve_chain")
        pool_chain = sem("pool_chain")
        rows_in = [sem(f"rows_in_{k}") for k in range(3)]
        top_in = [[sem(f"top_in_{k}_{c}") for c in range(2)] for k in range(3)]
        scores_mm = sem("scores_mm")
        exp_done = sem("exp_done")
        diag_done = sem("diag_done")
        values_mm = sem("values_mm")
        sum_set = sem("sum_set")
        sum_out = pair_of("sum_out")
        rot_mm = sem("rot_mm")
        rot_free = sem("rot_free")
        top_set = sem("top_set")
        top_part_set = sem("top_part_set")
        v_unit_set = sem("v_unit_set")
        bo_added = sem("bo_added")
        attn_in = pair_of("attn_in")
        sums_in = sem("sums_in")
        inv_set = sem("inv_set")
        inv_out = sem("inv_out")
        attn_set = sem("attn_set")
        proj_mm = sem("proj_mm")
        moments3 = sem("moments3")
        rstd3 = sem("rstd3")
        xn3 = sem("xn3")
        xn_turned = sem("xn_turned")
        xn_t3 = sem("xn_t3")
        logit_mm = sem("logit_mm")
        best_set = sem("best_set")
        tanh_set = sem("tanh_set")
        chosen_set = sem("chosen_set")
        picked_set = sem("picked_set")
        xs_set = sem("xs_set")
        xs_turned = sem("xs_turned")
        xs_t_set = sem("xs_t_set")
        gate_mm = sem("gate_mm")
        up_mm = sem("up_mm")
        pick_mm = sem("pick_mm")
        silu_set = sem("silu_set")
        hidden_set = sem("hidden_set")
        gated_set = sem("gated_set")
        down_mm = sem("down_mm")
        y_set = sem("y_set")
        y_out = pair_of("y_out")

        def hold(eng, s, value):
            eng.wait_ge(s, value)
            if not isinstance(value, int):
                eng.sem_inc(held, 1)

        class Chain:
            def __init__(self, eng, s):
                self.eng, self.s, self.base, self.n = eng, s, 0, 0

            def link(self, ins):
                self.n += 1
                ins.then_inc(self.s, 1)
                hold(self.eng, self.s, self.base + self.n)

        def looped(eng, count, body, per_iteration, chain=None):
            start = chain.n if chain else 0
            with eng.Fori(0, count) as i:
                if chain:
                    chain.base, chain.n = i * per_iteration, start
                body(i)
                if chain:
                    assert chain.n == start + per_iteration, (chain.n, start)
            if chain:
                chain.base, chain.n = 0, start + count * per_iteration

        LOOPS = (UNITS - 1) // 3
        FULL = unit_order(True, True)
        LEAD = unit_order(True, False)
        TAIL = unit_order(False, True)
        assert len(uses(FULL)) == ROT and len(uses(LEAD)) == FIRST

        def at(per, t, k, more=0):
            return t * (3 * per) + (per * k + more)

        def rot(t, k, r):
            return at(ROT, t, k, FIRST + r)

        def rot_before(r):
            return r - 3 if r >= 3 else (-2, -1, -3)[r]

        block = ctx.enter_context(nc.Block())

        @block.sync
        def _(sp):
            for s in split_out + sum_out + y_out + [s for k in top_in for s in k]:
                sp.sem_inc(s, 16)

            def load_x(n):
                sp.dma_start(x_sb[:, bass.ds(n * TPH, TPH), :],
                             x_tiles[:, bass.ds(n * TPH, TPH), :]).then_inc(x_in, 16)

            load_x(0)
            for dst, src in ((w_qkv[:, 0, :], wq_t), (w_qkv[:, 1, :], wk_t), (w_qkv[:, 2, :], wv_t),
                             (b_qk[:, 0:1], bq), (b_qk[:, 1:2], bk)):
                sp.dma_start(dst, src).then_inc(qkv_in, 16)
            with sp.Fori(1, STEPS) as n:
                sp.wait_ge(x_in, n * 16)
                load_x(n)

            def send_parts(b, h):
                sp.wait_ge(part3_set[h], b + 2)
                sp.dma_start(split[:, :, bass.ds(b * GH, GH), :, :]
                             .rearrange("s n u d (g t) -> (u d g) (s n) t", g=GH)
                             [:, :, h * HALF:(h + 1) * HALF],
                             part[:, h, :, :, :].rearrange("p s n t -> p (s n) t")
                             ).then_inc(split_out[h], 16)

            def load_rows(u, k):
                for first_row, n in PART_ROWS:
                    q_part = {3: 0, 2: 1, 1: 2}[n]
                    rows = slice(first_row * HD, (first_row + n) * HD)
                    sp.dma_start(q_rows[rows, k, :, :],
                                 split[0, q_part:q_part + 1, bass.ds(u, 1), :, :]
                                 .rearrange("n u d t -> (n u) d t").to_broadcast((n, HD, GH * SEQ))
                                 ).then_inc(rows_in[k], 16)
                    sp.dma_start(k_rows[rows, k, :, :],
                                 split[1, 0:n, bass.ds(u, 1), :, :]
                                 .rearrange("n u d t -> n (u d) t")).then_inc(rows_in[k], 16)
                sp.dma_start(q_rows[ROWS:ROWS_M, k, :, :],
                             q_rows[ROWS_M:ROWS_M + 3, k, :, :]).then_inc(rows_in[k], 16)

            def send_top(t, k, c):
                sp.dma_start(q_rows[ROWS:ROWS_M, k, :, c * HALF:(c + 1) * HALF],
                             top_rows[:, c, :]).then_inc(top_in[k][c], 16)

            def send_sums(t, k, c):
                sp.wait_ge(sum_set, at(2, t, k, c + 2))
                for g in range(GH):
                    sp.dma_start(sums[bass.ds(at(1, t, k), 1), g, :, c * HALF:(c + 1) * HALF],
                                 sum_sb[32 * g:32 * g + HD + 1, c, :]).then_inc(sum_out[c], 16)

            def turn_use(order, c, nxt):
                return [n for n, e in enumerate(uses(order)) if e == ("turn", c, nxt)][0]

            for h in range(2):
                send_parts(0, h)
            for h in range(2):
                sp.wait_ge(split_out[h], 32)
            sp.wait_ge(q_rows_set, 1)
            sp.wait_ge(k_rows_set, 1)
            load_rows(0, 0)
            with sp.Fori(1, BATCH) as b:
                for h in range(2):
                    send_parts(b, h)
            sp.wait_ge(k_rows_set, 3)
            load_rows(1, 1)
            for dst, src in ((b_v[:], bv), (b_o[:], bo.to_broadcast((P, DIM))),
                             (w_o[:], wo_t), (w_gate[:], gate_t), (w_g[:], wg_t), (w_u[:], wu_t),
                             (w_d[:], wd_t.rearrange("(q r) f -> r q f", q=PAIRS))):
                sp.dma_start(dst, src).then_inc(weights_in, 16)
            for h in range(2):
                sp.wait_ge(split_out[h], 16 * BATCH + 16)

            sp.wait_ge(rot_free, turn_use(LEAD, 0, 1) + 1)
            send_top(0, 0, 0)

            def step(t, k, load, rows):
                nt, nk = (t, k + 1) if k < 2 else (t + 1, 0)
                lt, lk = (t, k + 2) if k < 1 else (t + 1, k - 1)
                order = FULL if rows else TAIL
                sp.wait_ge(rot_free, rot(t, k, turn_use(order, 1, 0) + 1))
                send_top(t, k, 1)
                if load:
                    sp.wait_ge(scores_mm, at(24, t, k, 1))
                    load_rows(at(1, lt, lk), lk)
                send_sums(t, k, 0)
                if rows:
                    sp.wait_ge(rot_free, rot(t, k, turn_use(order, 0, 1) + 1))
                    send_top(nt, nk, 0)
                send_sums(t, k, 1)

            with sp.Fori(0, LOOPS - 1) as t:
                for k in range(3):
                    step(t, k, True, True)
            for k in range(3):
                step(LOOPS - 1, k, k < 2, True)
            step(LOOPS, 0, False, False)
            for c in range(2):
                sp.wait_ge(sum_out[c], 64 * UNITS + 16)

            sp.dma_start(sums_all, sums[:, :, HD, :].rearrange("u g t -> (u g) t")).then_inc(sums_in, 16)
            sp.wait_ge(inv_set, 1)
            sp.dma_start(inverse, sums_all).then_inc(inv_out, 16)
            sp.wait_ge(inv_out, 16)

            def load_attn(b, h):
                tokens = slice(h * HALF, (h + 1) * HALF)
                sp.dma_start(numer[:, h, :], sums[bass.ds(b * GH, GH), :, 0:HD, tokens]
                             .rearrange("u g d t -> (u g) d t")).then_inc(attn_in[h], 16)
                sp.dma_start(denom[:, h, :], inverse[bass.ds(b * HEADS, HEADS), None, tokens]
                             .to_broadcast((HEADS, HD, HALF))).then_inc(attn_in[h], 16)

            def store(t, h):
                sp.wait_ge(y_set, t * 2 + (h + 2))
                sp.dma_start(out_tiles[:, bass.ds(t * (2 * TPH) + h * TPH, TPH), :],
                             y[:, h, :, :]).then_inc(y_out[h], 16)

            load_attn(0, 0)
            load_attn(0, 1)
            with sp.Fori(0, BATCH - 1) as t:
                for h in range(2):
                    sp.wait_ge(attn_set, t * 2 + (h + 1))
                    load_attn(t + 1, h)
                    store(t, h)
            for h in range(2):
                store(BATCH - 1, h)
            for h in range(2):
                sp.wait_ge(y_out[h], 16 * BATCH + 16)

        @block.gpsimd
        def _(pool):
            chain = Chain(pool, pool_chain)
            g = nc.gpsimd
            for s in part3_set:
                pool.sem_inc(s, 1)
            chain.link(g.memset(ident[:], 0.0))
            chain.link(g.affine_select(out=ident[:], in_=ident[:], pattern=[[-1, P]], base=0,
                                       channel_multiplier=1, compare_op=ALU.not_equal, fill=1.0))
            g.tensor_copy(ident_b[:], ident[:]).then_inc(const_set, 1)
            g.memset(minus_half[:], -0.5).then_inc(const_set, 1)
            chain.link(g.memset(causal[:], 0.0))
            g.affine_select(out=causal[:, HALF - P:], in_=causal[:, HALF - P:], pattern=[[-1, P]], base=0,
                            channel_multiplier=1, compare_op=ALU.is_ge, fill=MASKED).then_inc(const_set, 1)
            for e in range(EXPERTS):
                last = g.memset(ramp[:, :, e:e + 1], float(EXPERTS - e))
            last.then_inc(const_set, 1)
            g.memset(k_rows[:, 0], -1.0).then_inc(k_rows_set, 1)

            def rsqrt(h, dst_sem):
                chain.link(g.tensor_scalar(spread[:, h, :], moments[:, h, :, 1], EPS, None, ALU.add))
                g.tensor_tensor(rstd[:, h, :], spread[:, h, :], minus_half[:], ALU.pow).then_inc(dst_sem, 1)

            pool.wait_ge(const_set, 4)

            def rsqrt1(b, h):
                hold(pool, moments_set[h], b + 1)
                rsqrt(h, rstd_set[h])

            def third(b, h):
                hold(pool, part2_set[h], b + 2)
                g.tensor_tensor(part[:, h, :, 2, :], rest[:, h, :, :], part[:, h, :, 1, :],
                                ALU.subtract).then_inc(part3_set[h], 1)

            rsqrt1(0, 0)
            rsqrt1(0, 1)

            def two_steps(t):
                for h in range(2):
                    rsqrt1(t + 1, h)
                    third(t, h)
            looped(pool, BATCH - 1, two_steps, 2, chain)
            third(BATCH - 1, 0)
            third(BATCH - 1, 1)
            for k in range(1, 3):
                g.memset(k_rows[:, k], -1.0).then_inc(k_rows_set, 1)
            chain.link(g.memset(v_unit[:], 0.0))
            g.memset(v_unit[:, :, :, :, HD:HD + 1], 1.0).then_inc(v_ones_set, 1)

            for h in range(2):
                pool.wait_ge(v_set[h], BATCH + 1)

            def copy_v(u, k):
                g.tensor_copy(v_unit[:, k, :, :, 0:HD], v_sb[:, bass.ds(u, 1), :, :, :]
                              .rearrange("p u j g d -> p (u j) g d")).then_inc(v_unit_set, 1)

            pool.wait_ge(v_ones_set, 1)
            copy_v(0, 0)

            def split_top(c):
                src = top_a[:, 0:TPH, :] if c == 0 else top[:]
                chain.link(g.tensor_copy(top_part[:, c, :, 0, :], src))
                chain.link(g.tensor_tensor(top_rest[:, c], src, top_part[:, c, :, 0, :], ALU.subtract))
                chain.link(g.tensor_copy(top_part[:, c, :, 1, :], top_rest[:, c]))
                g.tensor_tensor(top_part[:, c, :, 2, :], top_rest[:, c], top_part[:, c, :, 1, :],
                                ALU.subtract).then_inc(top_part_set, 1)

            pool.wait_ge(rot_free, 16)
            split_top(0)

            def add_bo(i):
                for j in range(TPH):
                    last = g.tensor_tensor(x_sb[:, bass.ds(i * TPH + j, 1), :],
                                           x_sb[:, bass.ds(i * TPH + j, 1), :], b_o[:, None, :], ALU.add)
                last.then_inc(bo_added, 1)
            pool.wait_ge(weights_in, 16 * 7)
            with pool.Fori(0, STEPS) as i:
                add_bo(i)

            pool.wait_ge(top_set, 1)
            split_top(1)

            def step(t, k, rows):
                nt, nk = (t, k + 1) if k < 2 else (t + 1, 0)
                order = FULL if rows else TAIL
                r, d = 0, 0
                for e in order:
                    if e[0] in ("piece", "turn"):
                        r += 1
                    if e == ("piece", ENDS[0] + 2):
                        hold(pool, rot_free, rot(t, k, r - 2))
                        split_top(0)
                    if e[0] == "scores" and e[1] in DIAG:
                        i, p = e[1], e[2]
                        hold(pool, exp_done, at(24, t, k, 2 + 2 * i + p + 1))
                        blockv = prob[:, i % 3, 2 * p:2 * p + 2, 0:P]
                        g.affine_select(out=blockv, in_=blockv, pattern=[[0, 2], [1, P]], base=0,
                                        channel_multiplier=-1, compare_op=ALU.is_ge,
                                        fill=0.0).then_inc(diag_done, 1)
                        if rows and i == 8 and p == 0:
                            hold(pool, values_mm, at(12, t, k, 3 + 1))
                            copy_v(at(1, nt, nk), nk)
                if rows:
                    hold(pool, top_set, at(1, t, k, 2))
                    split_top(1)

            def three(t):
                for k in range(3):
                    step(t, k, True)
            looped(pool, LOOPS, three, 18, chain)
            step(LOOPS, 0, False)

            def weigh(b, h):
                hold(pool, attn_in[h], b * 32 + 32)
                chain.link(g.tensor_tensor(attn[:, h, :], numer[:, h, :], denom[:, h, :], ALU.mult))
                g.tensor_scalar(attn[:, h, :], attn[:, h, :], b_v[:], None, ALU.add).then_inc(attn_set, 1)

            def pick(n, h):
                hold(pool, chosen_set, n)
                g.tensor_copy(picked[:, h].rearrange("p n (e i) -> p (n e) i", e=EXPERTS),
                              chosen[:, h].rearrange("p n e -> p (n e)")[:, :, None]
                              .to_broadcast((P, TPH * EXPERTS, INNER))).then_inc(picked_set, 1)

            def rsqrt3(n, h):
                hold(pool, moments3, n)
                rsqrt(h, rstd3)

            weigh(0, 0)
            rsqrt3(1, 0)
            weigh(0, 1)
            pick(1, 0)
            rsqrt3(2, 1)

            def two(t):
                for h in range(2):
                    weigh(t + 1, h)
                    pick(t * 2 + (h + 2), 1 - h)
                    rsqrt3(t * 2 + (h + 3), h)
            looped(pool, BATCH - 1, two, 4, chain)
            pick(STEPS, 1)

        @block.scalar
        def _(act):
            a = nc.scalar
            for s in xn_t_set + qk_set + v_set + [sum_set]:
                act.sem_inc(s, 1)
            act.wait_ge(qkv_in, 16 * 5)

            def copy_xn(b, h):
                act.wait_ge(turned[h], b + 2)
                act.wait_ge(v_mm[h], b + 1)
                a.activation(xn_t[:, h, :], ps[:, 4 * h, :], ACT.Copy).then_inc(xn_t_set[h], 1)

            def copy_qkv(b, h):
                act.wait_ge(qk_mm[h], b + 1)
                act.wait_ge(part2_set[h], b + 1)
                for side in range(2):
                    a.activation(qk[:, h, side, :], ps[:, 4 * h + 1 + side, :], ACT.Identity,
                                 bias=b_qk[:, side:side + 1])
                act.wait_ge(split_out[h], b * 16 + 16)
                for side in range(2):
                    last = a.activation(part[:, h, side, 0, :], ps[:, 4 * h + 1 + side, :], ACT.Identity,
                                        bias=b_qk[:, side:side + 1])
                last.then_inc(qk_set[h], 1)
                hold(act, v_mm[h], b + 2)
                a.activation(v_sb[:, bass.ds(b * GH, GH), h * TPH:(h + 1) * TPH, :, :]
                             .rearrange("p u j g d -> p u j (g d)"),
                             ps[:, 4 * h + 3, :].rearrange("p (j u f) -> p u j f", j=TPH, u=GH),
                             ACT.Copy).then_inc(v_set[h], 1)

            copy_xn(0, 0)
            with act.Fori(0, BATCH - 1) as t:
                copy_qkv(t, 0)
                copy_xn(t, 1)
                copy_qkv(t, 1)
                copy_xn(t + 1, 0)
            copy_qkv(BATCH - 1, 0)
            copy_xn(BATCH - 1, 1)
            copy_qkv(BATCH - 1, 1)

            act.sem_inc(exp_done, 2)
            chunk_end = {LAST[0] + 1: 0}

            def take_sums(t, k, c):
                act.wait_ge(values_mm, at(12, t, k, 3 + LAST[c] + 1))
                act.wait_ge(sum_out[c], at(64, t, k, 16))
                a.activation(sum_sb[:, c, :], ps[:, BANK_V, :], ACT.Copy).then_inc(sum_set, 1)

            def step(t, k):
                for i, (c, j, q0, n) in enumerate(SLOTS):
                    for p in range(2):
                        e = 2 * i + p
                        act.wait_ge(scores_mm, at(24, t, k, e + 1))
                        if p == 0:
                            act.wait_ge(values_mm, at(12, t, k, i + 1))
                        a.activation(prob[:, i % 3, 2 * p:2 * p + 2, 0:n],
                                     ps[:, 2 * (e % 2):2 * (e % 2) + 2, 0:n], ACT.Exp,
                                     scale=SCALE).then_inc(exp_done, 1)
                    if i in chunk_end:
                        take_sums(t, k, chunk_end[i])
                take_sums(t, k, 1)

            with act.Fori(0, LOOPS) as t:
                for k in range(3):
                    step(t, k)
            step(LOOPS, 0)

            def copy_xn3(n, h):
                act.wait_ge(xn_turned, n)
                a.activation(xn_t[:, h, :], ps[:, 1, :], ACT.Copy).then_inc(xn_t3, 1)

            def tanh(n, h):
                act.wait_ge(best_set, n)
                a.activation(weight[:, h, :], best[:, h, :], ACT.Tanh, scale=0.5).then_inc(tanh_set, 1)

            def copy_xs(n, h):
                act.wait_ge(xs_turned, n)
                a.activation(xs_t[:, h, :], ps[:, 1, :], ACT.Copy).then_inc(xs_t_set, 1)

            def back(n4, pr):
                act.wait_ge(gate_mm, n4 + (pr + 1))
                act.wait_ge(gated_set, n4 + (pr + 1))
                a.activation(silu[:, pr % 2, :], ps[:, 2 + pr % 2, :], ACT.Silu).then_inc(silu_set, 1)

            act.sem_inc(silu_set, 2)
            copy_xn3(1, 0)
            tanh(1, 0)
            copy_xs(1, 0)

            def steps(n4, n, h, more=True):
                back(n4, 0)
                if more:
                    copy_xn3(n + 1, 1 - h)
                back(n4, 1)
                if more:
                    tanh(n + 1, 1 - h)
                back(n4, 2)
                back(n4, 3)
                if more:
                    copy_xs(n + 1, 1 - h)

            with act.Fori(0, BATCH - 1) as t:
                for h in range(2):
                    steps(t * 8 + 4 * h, t * 2 + (h + 1), h)
            steps(8 * (BATCH - 1), STEPS - 1, 0)
            steps(8 * (BATCH - 1) + 4, STEPS, 1, False)

        @block.vector
        def _(dve):
            chain = Chain(dve, dve_chain)
            v = nc.vector
            for s in part2_set + [y_set, hidden_set]:
                dve.sem_inc(s, 1)
            v.memset(q_rows[:].rearrange("p k g t -> p (k g t)").bitcast(FP32), 0.0).then_inc(q_rows_set, 1)

            def count_moments(src, h, done):
                for i in range(TPH):
                    last = v.bn_stats(stats[:, h, i, :], src(i))
                chain.link(last)
                for i in range(TPH):
                    last = v.bn_aggr(moments[:, h, i, :], stats[:, h, i, :])
                last.then_inc(done, 1)

            def normalise(src, h, done):
                for i in range(TPH):
                    last = v.tensor_scalar(xn[:, h, i, :], src(i), moments[:, h, i, 0:1], rstd[:, h, i:i + 1],
                                           ALU.subtract, ALU.mult)
                last.then_inc(done, 1)

            def x_of(b, h):
                return lambda i: x_sb[:, bass.ds(b * (2 * TPH) + h * TPH + i, 1), :].rearrange("p n f -> p (n f)")

            def measure(b, h):
                hold(dve, x_in, b * 32 + 16 * (h + 1))
                count_moments(x_of(b, h), h, moments_set[h])

            def scale(b, h):
                hold(dve, turned[h], b + 1)
                hold(dve, rstd_set[h], b + 1)
                normalise(x_of(b, h), h, xn_set[h])

            def take_parts(b, h):
                hold(dve, split_out[h], b * 16 + 16)
                hold(dve, part3_set[h], b + 1)
                hold(dve, qk_set[h], b + 2)
                chain.link(v.tensor_tensor(rest[:, h, :, :], qk[:, h, :, :], part[:, h, :, 0, :],
                                           ALU.subtract))
                v.tensor_copy(part[:, h, :, 1, :], rest[:, h, :, :]).then_inc(part2_set[h], 1)

            measure(0, 0)
            measure(0, 1)
            scale(0, 0)

            def phase1(t):
                measure(t + 1, 0)
                scale(t, 1)
                take_parts(t, 0)
                measure(t + 1, 1)
                scale(t + 1, 0)
                take_parts(t, 1)
            looped(dve, BATCH - 1, phase1, 4, chain)
            scale(BATCH - 1, 1)
            take_parts(BATCH - 1, 0)
            take_parts(BATCH - 1, 1)
            dve.wait_ge(const_set, 4)

            def piece(n, bank):
                qt, head, k0, cols, diag = PIECES[n]
                if diag:
                    return v.tensor_tensor_reduce(
                        out=junk[:, bank, 0:cols], in0=ps[:, 5 + bank, 0:cols], in1=causal[:, HALF - cols:],
                        scale=1.0, scalar=-3e38, op0=ALU.add, op1=ALU.max,
                        accum_out=top_a[:, qt, head:head + 1])
                return v.tensor_reduce(top_b[:, qt - TPH, head:head + 1], ps[:, 5 + bank, 0:cols], AX.X, ALU.max)

            def turn(c, bank):
                src = ps[0:12, 5 + bank, :].bitcast(BF16)[:, 0:HALF]
                return v.tensor_copy(top_rows[:, c, :], src)

            def join(count):
                hold(dve, rot_free, count)
                v.tensor_tensor(top[:], top_a[:, TPH:, :], top_b[:], ALU.max).then_inc(top_set, 1)

            for r, e in enumerate(uses(LEAD)):
                dve.wait_ge(rot_mm, r + 1)
                bank = (r + 1) % 3
                ins = piece(e[1], bank) if e[0] == "piece" else turn(e[1], bank)
                ins.then_inc(rot_free, 1)
            join(FIRST)

            def step(t, k, rows):
                order = uses(FULL if rows else TAIL)
                kb, tb = (k - 1, t) if k else (2, t - 1)
                for r, e in enumerate(order):
                    if e[0] == "turn" and e[1] == 1:
                        hold(dve, top_in[kb][1], (tb + 1) * 16 + 16)
                    if e[0] == "turn" and e[1] == 0:
                        hold(dve, top_in[k][0], t * 16 + 32)
                    hold(dve, rot_mm, rot(t, k, r + 1))
                    ins = piece(e[1], r % 3) if e[0] == "piece" else turn(e[1], r % 3)
                    ins.then_inc(rot_free, 1)
                if rows:
                    join(rot(t, k, len(order)))

            with dve.Fori(0, LOOPS) as t:
                for k in range(3):
                    step(t, k, True)
            step(LOOPS, 0, False)

            dve.wait_ge(sums_in, 16)
            v.reciprocal(sums_all, sums_all).then_inc(inv_set, 1)

            def x1_of(b, h):
                return x_sb[:, bass.ds(b * (2 * TPH) + h * TPH, TPH), :]

            def residual(n, b, h):
                hold(dve, bo_added, n)
                hold(dve, proj_mm, n)
                chain.link(v.tensor_tensor(x1_of(b, h), ps[:, 0, :].rearrange("p (n f) -> p n f", n=TPH),
                                           x1_of(b, h), ALU.add))
                count_moments(x_of(b, h), h, moments3)
                hold(dve, rstd3, n)
                normalise(x_of(b, h), h, xn3)

            def route(n, h):
                hold(dve, logit_mm, n)
                logits = ps[:, 7, 0:TPH * EXPERTS].rearrange("p (n e) -> p n e", n=TPH)
                v.tensor_reduce(best[:, h, :], logits, AX.X, ALU.max).then_inc(best_set, 1)
                hold(dve, best_set, n)
                chain.link(v.tensor_tensor(hit[:, h], logits,
                                           best[:, h, :, None].to_broadcast((P, TPH, EXPERTS)), ALU.is_equal))
                chain.link(v.tensor_tensor(hit[:, h], hit[:, h], ramp[:], ALU.mult))
                chain.link(v.tensor_reduce(first[:, h, :], hit[:, h], AX.X, ALU.max))
                v.tensor_tensor(chosen[:, h], hit[:, h],
                                first[:, h, :, None].to_broadcast((P, TPH, EXPERTS)),
                                ALU.is_equal).then_inc(chosen_set, 1)
                hold(dve, tanh_set, n)
                chain.link(v.tensor_scalar(weight[:, h, :], weight[:, h, :], 0.5, 0.5, ALU.mult, ALU.add))
                for i in range(TPH):
                    last = v.tensor_scalar(xs[:, h, i, :], xn[:, h, i, :], weight[:, h, i:i + 1], None, ALU.mult)
                last.then_inc(xs_set, 1)

            def back(n4, pr):
                hold(dve, up_mm, n4 + (pr + 1))
                hold(dve, silu_set, n4 + (pr + 3))
                v.tensor_tensor(gated[:, pr % 2, :], ps[:, 4 + pr % 2, :], silu[:, pr % 2, :],
                                ALU.mult).then_inc(gated_set, 1)
                hold(dve, gated_set, n4 + (pr + 3))
                hold(dve, pick_mm, n4 + (pr + 1))
                v.tensor_tensor(hidden[:, pr, :], ps[:, 6, :], gated[:, pr % 2, :],
                                ALU.mult).then_inc(hidden_set, 1)

            def finish(n, b, h):
                hold(dve, down_mm, n)
                hold(dve, y_out[h], b * 16 + 16)
                v.tensor_tensor(y[:, h, :, :], ps[:, 7, :].rearrange("p (n f) -> p n f", n=TPH),
                                x1_of(b, h), ALU.add).then_inc(y_set, 1)

            dve.sem_inc(gated_set, 2)
            residual(1, 0, 0)
            route(1, 0)
            residual(2, 0, 1)

            def steps(n4, n, b, h, nb=None, more=True):
                back(n4, 0)
                back(n4, 1)
                if more:
                    route(n + 1, 1 - h)
                back(n4, 2)
                back(n4, 3)
                if nb is not None:
                    residual(n + 2, nb, h)
                finish(n, b, h)

            def two(t):
                for h in range(2):
                    steps(t * 8 + 4 * h, t * 2 + (h + 1), t, h, t + 1)
            looped(dve, BATCH - 1, two, 12, chain)
            steps(8 * (BATCH - 1), STEPS - 1, BATCH - 1, 0)
            steps(8 * (BATCH - 1) + 4, STEPS, BATCH - 1, 1, None, False)

        @block.tensor
        def _(pe):
            mm = nc.tensor.matmul
            for s in turned + v_mm:
                pe.sem_inc(s, 1)
            pe.wait_ge(const_set, 4)
            pe.wait_ge(qkv_in, 16 * 5)

            def turn_tiles(src, bank):
                for i in range(TPH):
                    last = nc.tensor.transpose(ps[:, bank, i * P:(i + 1) * P], src[:, i, :], ident[:])
                return last

            def turn1(b, h):
                pe.wait_ge(xn_set[h], b + 1)
                pe.wait_ge(xn_t_set[h], b + 1)
                turn_tiles(xn[:, h], 4 * h).then_inc(turned[h], 1)

            def project(b, h):
                pe.wait_ge(xn_t_set[h], b + 2)
                pe.wait_ge(qk_set[h], b + 1)
                for side in range(2):
                    last = mm(ps[:, 4 * h + 1 + side, :], w_qkv[:, side, :], xn_t[:, h, :], start=True, stop=True)
                last.then_inc(qk_mm[h], 1)
                pe.wait_ge(v_set[h], b + 1)
                for i in range(TPH):
                    last = mm(ps[:, 4 * h + 3, i * P:(i + 1) * P], xn_t[:, h, i * P:(i + 1) * P],
                              w_qkv[:, 2, :], start=True, stop=True)
                last.then_inc(v_mm[h], 1)

            turn1(0, 0)
            with pe.Fori(0, BATCH - 1) as t:
                project(t, 0)
                turn1(t, 1)
                project(t, 1)
                turn1(t + 1, 0)
            project(BATCH - 1, 0)
            turn1(BATCH - 1, 1)
            project(BATCH - 1, 1)
            for h in range(2):
                pe.wait_ge(qk_set[h], BATCH + 1)
                pe.wait_ge(v_set[h], BATCH + 1)

            def rows_piece(n, k, bank):
                qt, head, k0, cols, _ = PIECES[n]
                return mm(ps[:, 5 + bank, 0:cols], q_rows[:, k, head, qt * P:(qt + 1) * P],
                          k_rows[:, k, head, k0:k0 + cols], start=True, stop=True)

            def turn_top(c, bank):
                bank_b = ps[0:12, 5 + bank, :].bitcast(BF16)
                for i in range(TPH):
                    last = nc.tensor.transpose(bank_b[:, i * P:(i + 1) * P],
                                               top_part[:, c, i].rearrange("p r g -> p (r g)"), ident_b[:])
                return last

            pe.wait_ge(rows_in[0], 112)
            for r, e in enumerate(uses(LEAD)):
                if r >= 3:
                    pe.wait_ge(rot_free, r - 2)
                if e[0] == "turn":
                    pe.wait_ge(top_part_set, 1)
                bank = (r + 1) % 3
                ins = rows_piece(e[1], 0, bank) if e[0] == "piece" else turn_top(0, bank)
                ins.then_inc(rot_mm, 1)

            def step(t, k, rows):
                nt, nk = (t, k + 1) if k < 2 else (t + 1, 0)
                r = 0
                first_piece = True
                for e in (FULL if rows else TAIL):
                    if e[0] == "scores":
                        i, p = e[1], e[2]
                        c, j, q0, n = SLOTS[i]
                        x0 = 2 * i + p
                        if p == 0 and j == 0:
                            pe.wait_ge(top_in[k][c], t * 16 + 32)
                        pe.wait_ge(exp_done, at(24, t, k, x0 + 1))
                        for s in range(2):
                            last = mm(ps[:, 2 * (x0 % 2) + s, 0:n],
                                      k_rows[:, k, 2 * p + s, j * P:(j + 1) * P],
                                      q_rows[:, k, 2 * p + s, c * HALF + q0:(c + 1) * HALF],
                                      start=True, stop=True)
                        last.then_inc(scores_mm, 1)
                    elif e[0] == "values":
                        i = e[1]
                        c, j, q0, n = SLOTS[i]
                        if i == 0:
                            pe.wait_ge(v_unit_set, at(1, t, k, 1))
                        if j == 0:
                            pe.wait_ge(sum_set, at(2, t, k, c + 1))
                        if i in DIAG:
                            pe.wait_ge(diag_done, at(2 * len(DIAG), t, k, 2 * DIAG.index(i) + 2))
                        else:
                            pe.wait_ge(exp_done, at(24, t, k, 2 + 2 * i + 2))
                        for g in range(GH):
                            last = mm(ps[32 * g:32 * g + 32, BANK_V, q0:HALF], v_unit[:, k, j, g, :],
                                      prob[:, i % 3, g, 0:n], start=(j == 0), stop=(i == LAST[c]))
                        last.then_inc(values_mm, 1)
                    else:
                        if e[0] == "piece" and first_piece:
                            pe.wait_ge(rows_in[nk], (nt + 1) * 112)
                            first_piece = False
                        if e[0] == "turn":
                            pe.wait_ge(top_part_set, at(2, t, k, 2 if e[1] else 3))
                        pe.wait_ge(rot_free, rot(t, k, rot_before(r) + 1))
                        ins = rows_piece(e[1], nk, r % 3) if e[0] == "piece" else turn_top(e[1], r % 3)
                        ins.then_inc(rot_mm, 1)
                        r += 1

            pe.sem_inc(values_mm, 3)
            with pe.Fori(0, LOOPS) as t:
                for k in range(3):
                    step(t, k, True)
            step(LOOPS, 0, False)
            pe.wait_ge(sum_set, 2 * UNITS + 1)
            pe.wait_ge(rot_free, FIRST + ROT * (UNITS - 1) + 1)

            pe.wait_ge(weights_in, 16 * 7)

            def project3(n, h):
                pe.wait_ge(attn_set, n)
                for i in range(TPH):
                    last = mm(ps[:, 0, i * P:(i + 1) * P], attn[:, h, i * P:(i + 1) * P], w_o[:],
                              start=True, stop=True)
                last.then_inc(proj_mm, 1)

            def turn_xn(n, h):
                pe.wait_ge(xn3, n)
                turn_tiles(xn[:, h], 1).then_inc(xn_turned, 1)

            def logits(n, h, before, bank_used=True):
                pe.wait_ge(xn_t3, n)
                if bank_used:
                    pe.wait_ge(y_set, before)
                for i in range(TPH):
                    last = mm(ps[:, 7, i * EXPERTS:(i + 1) * EXPERTS], xn_t[:, h, i * P:(i + 1) * P], w_gate[:],
                              start=True, stop=True)
                last.then_inc(logit_mm, 1)

            def turn_xs(n, h):
                pe.wait_ge(xs_set, n)
                turn_tiles(xs[:, h], 1).then_inc(xs_turned, 1)

            def back(n, n4, h, pr):
                if pr == 0:
                    pe.wait_ge(xs_t_set, n)
                    pe.wait_ge(picked_set, n)
                cols = slice(pr * P, (pr + 1) * P)
                pe.wait_ge(silu_set, n4 + (pr + 1))
                mm(ps[:, 2 + pr % 2, :], w_g[:, cols], xs_t[:, h, :], start=True, stop=True).then_inc(gate_mm, 1)
                pe.wait_ge(gated_set, n4 + (pr + 1))
                mm(ps[:, 4 + pr % 2, :], w_u[:, cols], xs_t[:, h, :], start=True, stop=True).then_inc(up_mm, 1)
                pe.wait_ge(hidden_set, n4 + (pr + 1))
                for i in range(TPH):
                    last = mm(ps[:, 6, i * P:(i + 1) * P], picked[:, h, i, cols],
                              ident_b[:], start=True, stop=True)
                last.then_inc(pick_mm, 1)

            def down(n, n4):
                pe.wait_ge(hidden_set, n4 + (PAIRS + 1))
                pe.wait_ge(y_set, n)
                for i in range(TPH):
                    for pr in range(PAIRS):
                        last = mm(ps[:, 7, i * P:(i + 1) * P], hidden[:, pr, i * P:(i + 1) * P], w_d[:, pr, :],
                                  start=(pr == 0), stop=(pr == PAIRS - 1))
                last.then_inc(down_mm, 1)

            project3(1, 0)
            turn_xn(1, 0)
            project3(2, 1)
            logits(1, 0, 0, False)
            turn_xs(1, 0)

            def steps(n, n4, h, after=True, more=True):
                back(n, n4, h, 0)
                if more:
                    turn_xn(n + 1, 1 - h)
                back(n, n4, h, 1)
                if more:
                    logits(n + 1, 1 - h, n)
                back(n, n4, h, 2)
                back(n, n4, h, 3)
                if after:
                    project3(n + 2, h)
                if more:
                    turn_xs(n + 1, 1 - h)
                down(n, n4)

            with pe.Fori(0, BATCH - 1) as t:
                for h in range(2):
                    steps(t * 2 + (h + 1), t * 8 + 4 * h, h)
            steps(STEPS - 1, 8 * (BATCH - 1), 0, False)
            steps(STEPS, 8 * (BATCH - 1) + 4, 1, False, False)


def kernel(L0_attn_x, L0_attn_Wq, L0_attn_bq, L0_attn_Wk, L0_attn_bk, L0_attn_Wv, L0_attn_bv, L0_attn_Wo,
           L0_attn_bo, L0_ffn_gate_w, L0_ffn_w_gate, L0_ffn_w_up, L0_ffn_w_down):
    import numpy as np
    import concourse.bacc as bacc
    from concourse.bass_utils import run_bass_kernel_spmd

    def t(w):
        return np.ascontiguousarray(np.asarray(w).T)

    def by_unit(w):
        return np.ascontiguousarray(w.reshape(-1, HEADS // GH, GH, HD).transpose(0, 1, 3, 2)).reshape(-1, DIM)

    rows = EXPERTS * INNER
    given = {
        "x": np.asarray(L0_attn_x),
        "wq_t": by_unit(t(L0_attn_Wq)), "wk_t": by_unit(t(L0_attn_Wk)), "wv_t": t(L0_attn_Wv), "wo_t": t(L0_attn_Wo),
        "bq": by_unit(np.asarray(L0_attn_bq)).reshape(DIM, 1), "bk": by_unit(np.asarray(L0_attn_bk)).reshape(DIM, 1),
        "bv": np.asarray(L0_attn_bv).reshape(DIM, 1), "bo": np.asarray(L0_attn_bo).reshape(1, DIM),
        "gate_t": t(L0_ffn_gate_w),
        "wg_t": t(np.asarray(L0_ffn_w_gate).reshape(rows, DIM)),
        "wu_t": t(np.asarray(L0_ffn_w_up).reshape(rows, DIM)),
        "wd_t": np.ascontiguousarray(np.asarray(L0_ffn_w_down).transpose(0, 2, 1)).reshape(rows, DIM),
    }
    nc = bacc.Bacc("TRN2", target_bir_lowering=False, num_devices=1)
    args = [nc.dram_tensor(n, a.shape, FP32, kind="ExternalInput").ap() for n, a in given.items()]
    out = nc.dram_tensor("out", (BATCH, SEQ, DIM), FP32, kind="ExternalOutput").ap()
    layer_kernel(nc, *args, out)
    r = run_bass_kernel_spmd(nc, [given], core_ids=[0])
    return r.results[0]["out"]
```

```python
import concourse.bass as bass
from concourse import mybir
from contextlib import ExitStack

FP32 = mybir.dt.float32
BF16 = mybir.dt.bfloat16
ALU = mybir.AluOpType
ACT = mybir.ActivationFunctionType
AX = mybir.AxisListType

P = 128
BATCH, SEQ, DIM = 4, 1024, 128
HEADS, HD = 16, 8
EXPERTS, INNER = 8, 64
PAIRS = EXPERTS // 2
HALF = 512
TPH = HALF // P
TILES = BATCH * SEQ // P
STEPS = BATCH * SEQ // HALF
GH = 4
UNITS = BATCH * HEADS // GH
PART_ROWS = ((0, 3), (3, 2), (5, 1))
ROWS = 6 * HD
ROWS_M = ROWS + 3
INV_COLS = HEADS * SEQ // P
EPS = 1e-5
SCALE = float(HD) ** -0.5
MASKED = -1e30

SLOTS = [(c, j, max(0, P * j - HALF * c), HALF - max(0, P * j - HALF * c))
         for c in range(2) for j in range(TPH * (c + 1))]
DIAG = [i for i, (c, j, _, _) in enumerate(SLOTS) if j >= TPH * c]
LAST = {c: max(i for i, s in enumerate(SLOTS) if s[0] == c) for c in range(2)}
PIECES = []
for _qt in range(SEQ // P):
    for _g in range(GH):
        if _qt >= TPH:
            PIECES.append((_qt, _g, 0, HALF, False))
        PIECES.append((_qt, _g, HALF * (_qt // TPH), P * (_qt % TPH + 1), True))
ENDS = {c: max(i for i, s in enumerate(PIECES) if s[0] < TPH * (c + 1)) for c in range(2)}
ROT = len(PIECES) + 2
FIRST = len(PIECES) + 1


MERGED = ("SPPPSPPPSPaPSPPSPVPPSPVPPSSVPSPPSPVPSPPSPPV"
          "PSPSPPVPPSPPVPSbPPSPSPVPSPPSPSPVPSPSPVSPVPV")


def unit_order(rows, columns):
    if not columns:
        out = [("piece", n) for n in range(len(PIECES))]
        out.insert(ENDS[0] + 14, ("turn", 0, 1))
        return out
    seen = {"S": 0, "V": 0, "P": 0}
    out = []
    for letter in MERGED:
        n = seen.get(letter, 0)
        seen[letter] = n + 1
        if letter == "S":
            out.append(("scores", n // 2, n % 2))
        elif letter == "V":
            out.append(("values", n))
        elif letter == "a":
            out.append(("turn", 1, 0))
        elif rows:
            out.append(("piece", n) if letter == "P" else ("turn", 0, 1))
    assert seen["S"] == 2 * len(SLOTS) and seen["V"] == len(SLOTS) and seen["P"] == len(PIECES)
    return out


def uses(order):
    return [e for e in order if e[0] in ("piece", "turn")]


def layer_kernel(nc, x, wq_t, wk_t, wv_t, wo_t, bq, bk, bv, bo, gate_t, wg_t, wu_t, wd_t, out):
    split = nc.dram_tensor("split_parts", (2, 3, UNITS, HD, GH * SEQ), BF16, kind="Internal").ap()
    inverse = nc.dram_tensor("inverse_sums", (UNITS * GH, SEQ), FP32, kind="Internal").ap()
    sums = nc.dram_tensor("value_sums", (UNITS, GH, HD + 1, SEQ), FP32, kind="Internal").ap()
    x_tiles = x.rearrange("b (n p) f -> p (b n) f", p=P)
    out_tiles = out.rearrange("b (n p) f -> p (b n) f", p=P)

    ctx = ExitStack()
    with ctx:
        def sb(name, shape, dt=FP32):
            return ctx.enter_context(nc.sbuf_tensor(name, shape, dt))

        def sem(name):
            return ctx.enter_context(nc.semaphore(name))

        w_qkv = sb("w_qkv", [P, 3, DIM])
        w_o = sb("w_o", [P, DIM])
        w_gate = sb("w_gate", [P, EXPERTS])
        w_g = sb("w_g", [P, EXPERTS * INNER])
        w_u = sb("w_u", [P, EXPERTS * INNER])
        w_d = sb("w_d", [P, PAIRS, DIM])
        b_qk = sb("b_qk", [P, 2])
        b_v = sb("b_v", [P, 1])
        b_o = sb("b_o", [P, DIM])
        ident = sb("ident", [P, P])
        ident_b = sb("ident_b", [P, P], BF16)
        causal = sb("causal", [P, HALF])
        shut = sb("shut", [EXPERTS, EXPERTS * INNER], BF16)
        ramp = sb("ramp", [P, TPH, EXPERTS])
        minus_half = sb("minus_half", [P, TPH])
        x_sb = sb("x_sb", [P, TILES, DIM])
        v_sb = sb("v_sb", [P, UNITS, SEQ // P, GH, HD])
        stats = sb("stats", [P, 2, TPH, 6])
        moments = sb("moments", [P, 2, TPH, 2])
        spread = sb("spread", [P, 2, TPH])
        rstd = sb("rstd", [P, 2, TPH])
        xn = sb("xn", [P, 2, TPH, DIM])
        xn_t = sb("xn_t", [P, 2, HALF])
        qk = sb("qk", [P, 2, 2, HALF])
        rest = sb("rest", [P, 2, 2, HALF])
        part = sb("part", [P, 2, 2, 3, HALF], BF16)
        q_rows = sb("q_rows", [P, 3, GH, SEQ], BF16)
        k_rows = sb("k_rows", [P, 3, GH, SEQ], BF16)
        v_unit = sb("v_unit", [P, 3, SEQ // P, GH, 32])
        prob = sb("prob", [P, 3, GH, HALF])
        junk = sb("junk", [P, 3, HALF], BF16)
        top_a = sb("top_a", [P, SEQ // P, GH])
        top_b = sb("top_b", [P, TPH, GH])
        top = sb("top", [P, TPH, GH])
        top_rest = sb("top_rest", [P, 2, TPH, GH])
        top_part = sb("top_part", [P, 2, TPH, 3, GH], BF16)
        top_rows = sb("top_rows", [12, 2, HALF], BF16)
        sum_sb = sb("sum_sb", [P, 2, HALF])
        numer, denom = qk[:, 0, :, :], qk[:, 1, :, :]
        attn = rest[:, 0, :, :]
        inv = sb("inv", [P, BATCH, INV_COLS])
        best = sb("best", [P, 2, TPH])
        hit = sb("hit", [P, 2, TPH, EXPERTS])
        first = sb("first", [P, 2, TPH])
        refused = sb("refused", [P, 2, TPH, EXPERTS], BF16)
        refused_t = sb("refused_t", [EXPERTS, HALF], BF16)
        weight = sb("weight", [P, 2, TPH])
        xs = sb("xs", [P, 2, TPH, DIM])
        xs_t = sb("xs_t", [P, 2, HALF])
        hidden, silu = prob[:, 0, :, :], prob[:, 1, 0:2, :]
        y = sb("y", [P, 2, TPH, DIM])
        ps = ctx.enter_context(nc.psum_tensor("ps", [P, 8, HALF], FP32))
        BANK_V = 4
        BANK_PROJ, BANK_TURN, BANK_ROUTE, BANK_GATE, BANK_UP, BANK_DOWN = 5, 6, 7, 0, 2, 4

        weights_in = sem("weights_in")
        bias_in = sem("bias_in")
        bv_wide_set = sem("bv_wide_set")
        bias_mm = sem("bias_mm")
        bias_set = sem("bias_set")
        qkv_in = sem("qkv_in")
        x_in = sem("x_in")
        q_rows_set = sem("q_rows_set")
        q_zero_set = sem("q_zero_set")
        k_rows_set = sem("k_rows_set")
        const_set = sem("const_set")
        v_ones_set = sem("v_ones_set")
        held = sem("held")
        def pair_of(name):
            return [sem(name + "_0"), sem(name + "_1")]
        moments_set = pair_of("moments_set")
        rstd_set = pair_of("rstd_set")
        xn_set = pair_of("xn_set")
        turned = pair_of("turned")
        xn_t_set = pair_of("xn_t_set")
        qk_mm = pair_of("qk_mm")
        v_mm = pair_of("v_mm")
        qk_set = pair_of("qk_set")
        part2_set = pair_of("part2_set")
        part3_set = pair_of("part3_set")
        v_set = pair_of("v_set")
        split_out = pair_of("split_out")
        dve_chain = sem("dve_chain")
        pool_chain = sem("pool_chain")
        rows_in = [sem(f"rows_in_{k}") for k in range(3)]
        top_in = [[sem(f"top_in_{k}_{c}") for c in range(2)] for k in range(3)]
        scores_mm = sem("scores_mm")
        exp_done = sem("exp_done")
        diag_done = sem("diag_done")
        values_mm = sem("values_mm")
        sum_set = sem("sum_set")
        sum_out = pair_of("sum_out")
        rot_mm = sem("rot_mm")
        rot_free = sem("rot_free")
        top_set = sem("top_set")
        top_part_set = sem("top_part_set")
        v_unit_set = sem("v_unit_set")
        bo_added = sem("bo_added")
        attn_in = pair_of("attn_in")
        sums_in = sem("sums_in")
        inv_set = sem("inv_set")
        inv_out = sem("inv_out")
        attn_set = sem("attn_set")
        proj_mm = sem("proj_mm")
        moments3 = sem("moments3")
        rstd3 = sem("rstd3")
        xn3 = sem("xn3")
        xn_turned = sem("xn_turned")
        xn_t3 = sem("xn_t3")
        logit_mm = sem("logit_mm")
        best_set = sem("best_set")
        tanh_set = sem("tanh_set")
        refused_set = sem("refused_set")
        refused_turned = sem("refused_turned")
        refused_t_set = sem("refused_t_set")
        xs_set = sem("xs_set")
        xs_turned = sem("xs_turned")
        xs_t_set = sem("xs_t_set")
        gate_mm = sem("gate_mm")
        up_mm = sem("up_mm")
        silu_set = sem("silu_set")
        hidden_set = sem("hidden_set")
        down_mm = sem("down_mm")
        y_set = sem("y_set")
        y_out = pair_of("y_out")

        def hold(eng, s, value):
            eng.wait_ge(s, value)
            if not isinstance(value, int):
                eng.sem_inc(held, 1)

        class Chain:
            def __init__(self, eng, s):
                self.eng, self.s, self.base, self.n = eng, s, 0, 0

            def link(self, ins):
                self.n += 1
                ins.then_inc(self.s, 1)
                hold(self.eng, self.s, self.base + self.n)

        def looped(eng, count, body, per_iteration, chain=None):
            start = chain.n if chain else 0
            with eng.Fori(0, count) as i:
                if chain:
                    chain.base, chain.n = i * per_iteration, start
                body(i)
                if chain:
                    assert chain.n == start + per_iteration, (chain.n, start)
            if chain:
                chain.base, chain.n = 0, start + count * per_iteration

        LOOPS = (UNITS - 1) // 3
        FULL = unit_order(True, True)
        LEAD = unit_order(True, False)
        FRONT = (4, 7, 8)
        TAIL = unit_order(False, True)
        assert len(uses(FULL)) == ROT and len(uses(LEAD)) == FIRST

        def at(per, t, k, more=0):
            return t * (3 * per) + (per * k + more)

        def rot(t, k, r):
            return at(ROT, t, k, FIRST + r)

        def rot_before(r):
            return r - 3 if r >= 3 else (-2, -1, -3)[r]

        block = ctx.enter_context(nc.Block())

        @block.sync
        def _(sp):
            for s in split_out + sum_out + y_out + [s for k in top_in for s in k]:
                sp.sem_inc(s, 16)

            def load_x(n):
                sp.dma_start(x_sb[:, bass.ds(n * TPH, TPH), :],
                             x_tiles[:, bass.ds(n * TPH, TPH), :]).then_inc(x_in, 16)

            load_x(0)
            for dst, src in ((w_qkv[:, 0, :], wq_t), (w_qkv[:, 1, :], wk_t), (w_qkv[:, 2, :], wv_t),
                             (b_qk[:, 0:1], bq), (b_qk[:, 1:2], bk)):
                sp.dma_start(dst, src).then_inc(qkv_in, 16)
            for dst, src in ((b_v[:], bv), (w_o[:], wo_t), (b_o[:], bo.to_broadcast((P, DIM)))):
                sp.dma_start(dst, src).then_inc(bias_in, 16)
            with sp.Fori(1, STEPS) as n:
                sp.wait_ge(x_in, n * 16)
                load_x(n)

            def send_parts(b, h):
                sp.wait_ge(part3_set[h], b + 2)
                sp.dma_start(split[:, :, bass.ds(b * GH, GH), :, :]
                             .rearrange("s n u d (g t) -> (u d g) (s n) t", g=GH)
                             [:, :, h * HALF:(h + 1) * HALF],
                             part[:, h, :, :, :].rearrange("p s n t -> p (s n) t")
                             ).then_inc(split_out[h], 16)

            def load_rows(u, k):
                for first_row, n in PART_ROWS:
                    q_part = {3: 0, 2: 1, 1: 2}[n]
                    rows = slice(first_row * HD, (first_row + n) * HD)
                    sp.dma_start(q_rows[rows, k, :, :],
                                 split[0, q_part:q_part + 1, bass.ds(u, 1), :, :]
                                 .rearrange("n u d t -> (n u) d t").to_broadcast((n, HD, GH * SEQ))
                                 ).then_inc(rows_in[k], 16)
                    sp.dma_start(k_rows[rows, k, :, :],
                                 split[1, 0:n, bass.ds(u, 1), :, :]
                                 .rearrange("n u d t -> n (u d) t")).then_inc(rows_in[k], 16)
                sp.dma_start(q_rows[ROWS:ROWS_M, k, :, :],
                             q_rows[ROWS_M:ROWS_M + 3, k, :, :]).then_inc(rows_in[k], 16)

            def send_top(t, k, c):
                sp.dma_start(q_rows[ROWS:ROWS_M, k, :, c * HALF:(c + 1) * HALF],
                             top_rows[:, c, :]).then_inc(top_in[k][c], 16)

            def send_sums(t, k, c):
                sp.wait_ge(sum_set, at(2, t, k, c + 2))
                for g in range(GH):
                    sp.dma_start(sums[bass.ds(at(1, t, k), 1), g, :, c * HALF:(c + 1) * HALF],
                                 sum_sb[32 * g:32 * g + HD + 1, c, :]).then_inc(sum_out[c], 16)

            def turn_use(order, c, nxt):
                return [n for n, e in enumerate(uses(order)) if e == ("turn", c, nxt)][0]

            with sp.Fori(0, BATCH - 1) as b:
                for h in range(2):
                    send_parts(b, h)
            for h in range(2):
                sp.wait_ge(split_out[h], 32)
            sp.wait_ge(q_rows_set, 1)
            sp.wait_ge(k_rows_set, 1)
            load_rows(0, 0)
            for h in range(2):
                send_parts(BATCH - 1, h)
            sp.wait_ge(q_zero_set, 2)
            sp.wait_ge(k_rows_set, 3)
            load_rows(1, 1)
            for dst, src in ((w_gate[:], gate_t), (w_g[:], wg_t), (w_u[:], wu_t),
                             (w_d[:], wd_t.rearrange("(q r) f -> r q f", q=PAIRS))):
                sp.dma_start(dst, src).then_inc(weights_in, 16)
            for h in range(2):
                sp.wait_ge(split_out[h], 16 * BATCH + 16)

            sp.wait_ge(rot_free, turn_use(LEAD, 0, 1) + 1)
            send_top(0, 0, 0)

            def step(t, k, load, rows, between=None):
                nt, nk = (t, k + 1) if k < 2 else (t + 1, 0)
                lt, lk = (t, k + 2) if k < 1 else (t + 1, k - 1)
                order = FULL if rows else TAIL
                sp.wait_ge(rot_free, rot(t, k, turn_use(order, 1, 0) + 1))
                send_top(t, k, 1)
                if between:
                    between()
                if load:
                    sp.wait_ge(scores_mm, at(24, t, k, 1))
                    load_rows(at(1, lt, lk), lk)
                send_sums(t, k, 0)
                if rows:
                    sp.wait_ge(rot_free, rot(t, k, turn_use(order, 0, 1) + 1))
                    send_top(nt, nk, 0)
                send_sums(t, k, 1)

            with sp.Fori(0, LOOPS - 1) as t:
                for k in range(3):
                    step(t, k, True, True)

            def load_sums(b):
                sp.dma_start(inv[:, b, :], sums[b * GH:(b + 1) * GH, :, HD, :]
                             .rearrange("u g (c t) -> (u g) c t", t=INV_COLS)).then_inc(sums_in, 16)

            def store_inverse(b):
                sp.dma_start(inverse[b * HEADS:(b + 1) * HEADS, :]
                             .rearrange("h (c t) -> h c t", t=INV_COLS), inv[:, b, :]).then_inc(inv_out, 16)

            def load_attn(b, h):
                tokens = slice(h * HALF, (h + 1) * HALF)
                sp.dma_start(numer[:, h, :], sums[bass.ds(b * GH, GH), :, 0:HD, tokens]
                             .rearrange("u g d t -> (u g) d t")).then_inc(attn_in[h], 16)
                sp.dma_start(denom[:, h, :], inverse[bass.ds(b * HEADS, HEADS), None, tokens]
                             .to_broadcast((HEADS, HD, HALF))).then_inc(attn_in[h], 16)

            def first_attn():
                sp.wait_ge(inv_out, 16)
                load_attn(0, 0)
                load_attn(0, 1)
                for b in range(1, BATCH - 1):
                    store_inverse(b)

            for k in range(3):
                step(LOOPS - 1, k, k < 2, True)
                if k == 1:
                    for c in range(2):
                        sp.wait_ge(sum_out[c], 64 * GH * (BATCH - 1) + 16)
                    for b in range(BATCH - 1):
                        load_sums(b)
            sp.wait_ge(inv_set, 1)
            store_inverse(0)
            step(LOOPS, 0, False, False, first_attn)
            for c in range(2):
                sp.wait_ge(sum_out[c], 64 * UNITS + 16)

            load_sums(BATCH - 1)

            def store(t, h):
                sp.wait_ge(y_set, t * 2 + (h + 2))
                sp.dma_start(out_tiles[:, bass.ds(t * (2 * TPH) + h * TPH, TPH), :],
                             y[:, h, :, :]).then_inc(y_out[h], 16)

            def reload(t):
                for h in range(2):
                    sp.wait_ge(attn_set, t * 2 + (h + 1))
                    load_attn(t + 1, h)
                    store(t, h)

            sp.wait_ge(inv_out, 16 * (BATCH - 1))
            reload(0)
            sp.wait_ge(inv_set, 2)
            store_inverse(BATCH - 1)
            sp.wait_ge(inv_out, 16 * BATCH)
            with sp.Fori(1, BATCH - 1) as t:
                reload(t)
            for h in range(2):
                store(BATCH - 1, h)
            for h in range(2):
                sp.wait_ge(y_out[h], 16 * BATCH + 16)

        @block.gpsimd
        def _(pool):
            chain = Chain(pool, pool_chain)
            g = nc.gpsimd
            for s in part3_set:
                pool.sem_inc(s, 1)
            chain.link(g.memset(ident[:], 0.0))
            chain.link(g.affine_select(out=ident[:], in_=ident[:], pattern=[[-1, P]], base=0,
                                       channel_multiplier=1, compare_op=ALU.not_equal, fill=1.0))
            g.tensor_copy(ident_b[:], ident[:]).then_inc(const_set, 1)
            g.memset(minus_half[:], -0.5).then_inc(const_set, 1)
            chain.link(g.memset(causal[:], 0.0))
            g.affine_select(out=causal[:, HALF - P:], in_=causal[:, HALF - P:], pattern=[[-1, P]], base=0,
                            channel_multiplier=1, compare_op=ALU.is_ge, fill=MASKED).then_inc(const_set, 1)
            for e in range(EXPERTS):
                last = g.memset(ramp[:, :, e:e + 1], float(EXPERTS - e))
            last.then_inc(const_set, 1)
            chain.link(g.memset(shut[:], MASKED))
            chain.link(g.affine_select(out=shut[:], in_=shut[:], pattern=[[1, EXPERTS * INNER]], base=0,
                                       channel_multiplier=-INNER, compare_op=ALU.is_ge, fill=0.0))
            g.affine_select(out=shut[:], in_=shut[:], pattern=[[-1, EXPERTS * INNER]], base=INNER - 1,
                            channel_multiplier=INNER, compare_op=ALU.is_ge, fill=0.0).then_inc(const_set, 1)
            g.memset(k_rows[:, 0], -1.0).then_inc(k_rows_set, 1)

            def rsqrt(h, dst_sem):
                chain.link(g.tensor_scalar(spread[:, h, :], moments[:, h, :, 1], EPS, None, ALU.add))
                g.tensor_tensor(rstd[:, h, :], spread[:, h, :], minus_half[:], ALU.pow).then_inc(dst_sem, 1)

            pool.wait_ge(const_set, 5)

            def rsqrt1(b, h):
                hold(pool, moments_set[h], b + 1)
                rsqrt(h, rstd_set[h])

            def third(b, h):
                hold(pool, part2_set[h], b + 2)
                g.tensor_tensor(part[:, h, :, 2, :], rest[:, h, :, :], part[:, h, :, 1, :],
                                ALU.subtract).then_inc(part3_set[h], 1)

            rsqrt1(0, 0)
            rsqrt1(0, 1)
            rsqrt1(1, 0)

            def two_steps(t, more=True):
                rsqrt1(t + 1, 1)
                third(t, 0)
                if more:
                    rsqrt1(t + 2, 0)
                third(t, 1)
            looped(pool, BATCH - 2, two_steps, 2, chain)
            two_steps(BATCH - 2, False)
            third(BATCH - 1, 0)
            third(BATCH - 1, 1)
            for k in range(1, 3):
                g.memset(k_rows[:, k], -1.0).then_inc(k_rows_set, 1)
            chain.link(g.memset(v_unit[:], 0.0))
            g.memset(v_unit[:, :, :, :, HD:HD + 1], 1.0).then_inc(v_ones_set, 1)

            for h in range(2):
                pool.wait_ge(v_set[h], BATCH + 1)

            def copy_v(u, k):
                g.tensor_copy(v_unit[:, k, :, :, 0:HD], v_sb[:, bass.ds(u, 1), :, :, :]
                              .rearrange("p u j g d -> p (u j) g d")).then_inc(v_unit_set, 1)

            pool.wait_ge(v_ones_set, 1)
            copy_v(0, 0)

            def split_top(c):
                src = top_a[:, 0:TPH, :] if c == 0 else top[:]
                chain.link(g.tensor_copy(top_part[:, c, :, 0, :], src))
                chain.link(g.tensor_tensor(top_rest[:, c], src, top_part[:, c, :, 0, :], ALU.subtract))
                chain.link(g.tensor_copy(top_part[:, c, :, 1, :], top_rest[:, c]))
                g.tensor_tensor(top_part[:, c, :, 2, :], top_rest[:, c], top_part[:, c, :, 1, :],
                                ALU.subtract).then_inc(top_part_set, 1)

            pool.wait_ge(rot_free, 16)
            split_top(0)

            def add_bo(i):
                for j in range(TPH):
                    last = g.tensor_tensor(x_sb[:, bass.ds(i * TPH + j, 1), :],
                                           x_sb[:, bass.ds(i * TPH + j, 1), :], b_o[:, None, :], ALU.add)
                last.then_inc(bo_added, 1)
            pool.wait_ge(bias_set, 1)
            with pool.Fori(0, STEPS) as i:
                add_bo(i)

            pool.wait_ge(top_set, 1)
            split_top(1)

            def step(t, k, rows, between=None):
                nt, nk = (t, k + 1) if k < 2 else (t + 1, 0)
                order = FULL if rows else TAIL
                r = 0
                for e in order:
                    if between and e[0] == "values":
                        between(e[1])
                    if e[0] in ("piece", "turn"):
                        r += 1
                    if e == ("piece", ENDS[0] + 2):
                        hold(pool, rot_free, rot(t, k, r - 2))
                        split_top(0)
                    if e[0] == "scores" and e[1] in DIAG:
                        i, p = e[1], e[2]
                        hold(pool, exp_done, at(24, t, k, 2 + 2 * i + p + 1))
                        blockv = prob[:, i % 3, 2 * p:2 * p + 2, 0:P]
                        g.affine_select(out=blockv, in_=blockv, pattern=[[0, 2], [1, P]], base=0,
                                        channel_multiplier=-1, compare_op=ALU.is_ge,
                                        fill=0.0).then_inc(diag_done, 1)
                        if rows and i == 8 and p == 0:
                            hold(pool, values_mm, at(12, t, k, 3 + 1))
                            copy_v(at(1, nt, nk), nk)
                if rows:
                    hold(pool, top_set, at(1, t, k, 2))
                    split_top(1)

            def three(t):
                for k in range(3):
                    step(t, k, True)
            looped(pool, LOOPS, three, 18, chain)

            def weigh(b, h):
                hold(pool, attn_in[h], b * 32 + 32)
                g.tensor_tensor(attn[:, h, :], numer[:, h, :], denom[:, h, :], ALU.mult).then_inc(attn_set, 1)

            def rsqrt3(n, h):
                hold(pool, moments3, n)
                rsqrt(h, rstd3)

            def lead_in(i):
                if i == FRONT[0]:
                    weigh(0, 0)
                    weigh(0, 1)
                    rsqrt3(1, 0)

            step(LOOPS, 0, False, lead_in)
            rsqrt3(2, 1)

            def two(t):
                for h in range(2):
                    weigh(t + 1, h)
                    rsqrt3(t * 2 + (h + 3), h)
            looped(pool, BATCH - 1, two, 2, chain)

        @block.scalar
        def _(act):
            a = nc.scalar
            for s in xn_t_set + qk_set + v_set + [sum_set]:
                act.sem_inc(s, 1)
            act.wait_ge(const_set, 2)
            for k in range(1, 3):
                a.activation(q_rows[:, k].rearrange("p g t -> p (g t)").bitcast(FP32),
                             minus_half[:, 0:1].to_broadcast((P, GH * SEQ // 2)), ACT.Copy,
                             scale=0.0).then_inc(q_zero_set, 1)
            act.wait_ge(qkv_in, 16 * 5)

            def copy_xn(b, h):
                act.wait_ge(turned[h], b + 2)
                act.wait_ge(v_mm[h], b + 1)
                a.activation(xn_t[:, h, :], ps[:, 4 * h, :], ACT.Copy).then_inc(xn_t_set[h], 1)

            def copy_qkv(b, h):
                act.wait_ge(qk_mm[h], b + 1)
                act.wait_ge(part2_set[h], b + 1)
                for side in range(2):
                    a.activation(qk[:, h, side, :], ps[:, 4 * h + 1 + side, :], ACT.Identity,
                                 bias=b_qk[:, side:side + 1])
                act.wait_ge(split_out[h], b * 16 + 16)
                for side in range(2):
                    last = a.activation(part[:, h, side, 0, :], ps[:, 4 * h + 1 + side, :], ACT.Identity,
                                        bias=b_qk[:, side:side + 1])
                last.then_inc(qk_set[h], 1)
                hold(act, v_mm[h], b + 2)
                a.activation(v_sb[:, bass.ds(b * GH, GH), h * TPH:(h + 1) * TPH, :, :]
                             .rearrange("p u j g d -> p u j (g d)"),
                             ps[:, 4 * h + 3, :].rearrange("p (j u f) -> p u j f", j=TPH, u=GH),
                             ACT.Copy).then_inc(v_set[h], 1)

            copy_xn(0, 0)
            with act.Fori(0, BATCH - 1) as t:
                copy_xn(t, 1)
                copy_qkv(t, 0)
                copy_xn(t + 1, 0)
                copy_qkv(t, 1)
            copy_xn(BATCH - 1, 1)
            copy_qkv(BATCH - 1, 0)
            copy_qkv(BATCH - 1, 1)

            act.sem_inc(exp_done, 2)

            def take_sums(t, k, c):
                act.wait_ge(values_mm, at(12, t, k, 3 + LAST[c] + 1))
                act.wait_ge(sum_out[c], at(64, t, k, 16))
                a.activation(sum_sb[:, c, :], ps[:, BANK_V, :], ACT.Copy).then_inc(sum_set, 1)

            def step(t, k, between=None):
                for i, (c, j, q0, n) in enumerate(SLOTS):
                    for p in range(2):
                        e = 2 * i + p
                        act.wait_ge(scores_mm, at(24, t, k, e + 1))
                        if p == 0:
                            act.wait_ge(values_mm, at(12, t, k, i + 1))
                        a.activation(prob[:, i % 3, 2 * p:2 * p + 2, 0:n],
                                     ps[:, 2 * (e % 2):2 * (e % 2) + 2, 0:n], ACT.Exp,
                                     scale=SCALE).then_inc(exp_done, 1)
                    if i == LAST[0] + 1:
                        take_sums(t, k, 0)
                    if between:
                        between(i)
                take_sums(t, k, 1)

            with act.Fori(0, LOOPS) as t:
                for k in range(3):
                    step(t, k)

            def copy_xn3(n, h):
                act.wait_ge(xn_turned, n)
                a.activation(xn_t[:, h, :], ps[:, BANK_TURN, :], ACT.Copy).then_inc(xn_t3, 1)

            def tanh(n, h):
                act.wait_ge(best_set, n)
                a.activation(weight[:, h, :], best[:, h, :], ACT.Tanh, scale=0.5).then_inc(tanh_set, 1)

            def copy_refused(n):
                act.wait_ge(refused_turned, n)
                a.activation(refused_t[:], ps[0:EXPERTS, BANK_ROUTE, :].bitcast(BF16)[:, HALF:],
                             ACT.Copy).then_inc(refused_t_set, 1)

            def copy_xs(n, h):
                act.wait_ge(xs_turned, n)
                a.activation(xs_t[:, h, :], ps[:, BANK_TURN, :], ACT.Copy).then_inc(xs_t_set, 1)

            def lead_in(i):
                if i == FRONT[1] + 1:
                    copy_xn3(1, 0)
                if i == FRONT[2] + 1:
                    tanh(1, 0)

            step(LOOPS, 0, lead_in)

            def back(n4, pr):
                act.wait_ge(gate_mm, n4 + (pr + 1))
                act.wait_ge(hidden_set, n4 + (pr + 1))
                a.activation(silu[:, pr % 2, :], ps[:, BANK_GATE + pr % 2, :], ACT.Silu).then_inc(silu_set, 1)

            act.sem_inc(silu_set, 2)
            copy_refused(1)
            copy_xs(1, 0)

            def steps(n4, n, h, more=True):
                back(n4, 0)
                if more:
                    copy_xn3(n + 1, 1 - h)
                back(n4, 1)
                if more:
                    tanh(n + 1, 1 - h)
                back(n4, 2)
                back(n4, 3)
                if more:
                    copy_refused(n + 1)
                    copy_xs(n + 1, 1 - h)

            with act.Fori(0, BATCH - 1) as t:
                for h in range(2):
                    steps(t * 8 + 4 * h, t * 2 + (h + 1), h)
            steps(8 * (BATCH - 1), STEPS - 1, 0)
            steps(8 * (BATCH - 1) + 4, STEPS, 1, False)

        @block.vector
        def _(dve):
            chain = Chain(dve, dve_chain)
            v = nc.vector
            for s in part2_set + [y_set]:
                dve.sem_inc(s, 1)
            v.memset(q_rows[:, 0].rearrange("p g t -> p (g t)").bitcast(FP32), 0.0).then_inc(q_rows_set, 1)
            def count_moments(src, h, done):
                for i in range(TPH):
                    last = v.bn_stats(stats[:, h, i, :], src(i))
                chain.link(last)
                for i in range(TPH):
                    last = v.bn_aggr(moments[:, h, i, :], stats[:, h, i, :])
                last.then_inc(done, 1)

            def normalise(src, h, done):
                for i in range(TPH):
                    last = v.tensor_scalar(xn[:, h, i, :], src(i), moments[:, h, i, 0:1], rstd[:, h, i:i + 1],
                                           ALU.subtract, ALU.mult)
                last.then_inc(done, 1)

            def x_of(b, h):
                return lambda i: x_sb[:, bass.ds(b * (2 * TPH) + h * TPH + i, 1), :].rearrange("p n f -> p (n f)")

            def measure(b, h):
                hold(dve, x_in, b * 32 + 16 * (h + 1))
                count_moments(x_of(b, h), h, moments_set[h])

            def scale(b, h):
                hold(dve, turned[h], b + 1)
                hold(dve, rstd_set[h], b + 1)
                normalise(x_of(b, h), h, xn_set[h])

            def take_parts(b, h):
                hold(dve, split_out[h], b * 16 + 16)
                hold(dve, part3_set[h], b + 1)
                hold(dve, qk_set[h], b + 2)
                chain.link(v.tensor_tensor(rest[:, h, :, :], qk[:, h, :, :], part[:, h, :, 0, :],
                                           ALU.subtract))
                v.tensor_copy(part[:, h, :, 1, :], rest[:, h, :, :]).then_inc(part2_set[h], 1)

            measure(0, 0)
            measure(0, 1)
            scale(0, 0)
            dve.wait_ge(bias_in, 16 * 3)
            v.tensor_copy(xs[:, 0, 0, :], b_v[:].to_broadcast((P, DIM))).then_inc(bv_wide_set, 1)
            measure(1, 0)
            dve.wait_ge(bias_mm, 1)
            v.tensor_tensor(b_o[:], b_o[:], ps[:, 7, 0:DIM], ALU.add).then_inc(bias_set, 1)
            scale(0, 1)

            def phase1(t, more=True):
                measure(t + 1, 1)
                scale(t + 1, 0)
                take_parts(t, 0)
                if more:
                    measure(t + 2, 0)
                scale(t + 1, 1)
                take_parts(t, 1)
            looped(dve, BATCH - 2, phase1, 4, chain)
            phase1(BATCH - 2, False)
            take_parts(BATCH - 1, 0)
            take_parts(BATCH - 1, 1)
            dve.wait_ge(const_set, 5)

            def piece(n, bank):
                qt, head, k0, cols, diag = PIECES[n]
                if diag:
                    return v.tensor_tensor_reduce(
                        out=junk[:, bank, 0:cols], in0=ps[:, 5 + bank, 0:cols], in1=causal[:, HALF - cols:],
                        scale=1.0, scalar=-3e38, op0=ALU.add, op1=ALU.max,
                        accum_out=top_a[:, qt, head:head + 1])
                return v.tensor_reduce(top_b[:, qt - TPH, head:head + 1], ps[:, 5 + bank, 0:cols], AX.X, ALU.max)

            def turn(c, bank):
                src = ps[0:12, 5 + bank, :].bitcast(BF16)[:, 0:HALF]
                return v.tensor_copy(top_rows[:, c, :], src)

            def join(count):
                hold(dve, rot_free, count)
                v.tensor_tensor(top[:], top_a[:, TPH:, :], top_b[:], ALU.max).then_inc(top_set, 1)

            for r, e in enumerate(uses(LEAD)):
                dve.wait_ge(rot_mm, r + 1)
                bank = (r + 1) % 3
                ins = piece(e[1], bank) if e[0] == "piece" else turn(e[1], bank)
                ins.then_inc(rot_free, 1)
            join(FIRST)

            def step(t, k, rows):
                order = uses(FULL if rows else TAIL)
                kb, tb = (k - 1, t) if k else (2, t - 1)
                for r, e in enumerate(order):
                    if e[0] == "turn" and e[1] == 1:
                        hold(dve, top_in[kb][1], (tb + 1) * 16 + 16)
                    if e[0] == "turn" and e[1] == 0:
                        hold(dve, top_in[k][0], t * 16 + 32)
                    hold(dve, rot_mm, rot(t, k, r + 1))
                    ins = piece(e[1], r % 3) if e[0] == "piece" else turn(e[1], r % 3)
                    ins.then_inc(rot_free, 1)
                if rows:
                    join(rot(t, k, len(order)))

            with dve.Fori(0, LOOPS) as t:
                for k in range(3):
                    step(t, k, True)
            def invert(b0, b1):
                v.reciprocal(inv[:, b0:b1], inv[:, b0:b1]).then_inc(inv_set, 1)

            dve.wait_ge(sums_in, 16 * (BATCH - 1))
            invert(0, BATCH - 1)
            step(LOOPS, 0, False)

            def x1_of(b, h):
                return x_sb[:, bass.ds(b * (2 * TPH) + h * TPH, TPH), :]

            def residual(n, b, h):
                hold(dve, bo_added, n)
                hold(dve, proj_mm, n)
                chain.link(v.tensor_tensor(x1_of(b, h), ps[:, BANK_PROJ, :].rearrange("p (n f) -> p n f", n=TPH),
                                           x1_of(b, h), ALU.add))
                count_moments(x_of(b, h), h, moments3)
                hold(dve, rstd3, n)
                normalise(x_of(b, h), h, xn3)

            def route(n, h):
                hold(dve, logit_mm, n)
                logits = ps[:, BANK_ROUTE, 0:TPH * EXPERTS].rearrange("p (n e) -> p n e", n=TPH)
                v.tensor_reduce(best[:, h, :], logits, AX.X, ALU.max).then_inc(best_set, 1)
                hold(dve, best_set, n)
                chain.link(v.tensor_tensor(hit[:, h], logits,
                                           best[:, h, :, None].to_broadcast((P, TPH, EXPERTS)), ALU.is_equal))
                chain.link(v.tensor_tensor(hit[:, h], hit[:, h], ramp[:], ALU.mult))
                chain.link(v.tensor_reduce(first[:, h, :], hit[:, h], AX.X, ALU.max))
                v.tensor_tensor(refused[:, h], hit[:, h],
                                first[:, h, :, None].to_broadcast((P, TPH, EXPERTS)),
                                ALU.not_equal).then_inc(refused_set, 1)
                hold(dve, tanh_set, n)
                chain.link(v.tensor_scalar(weight[:, h, :], weight[:, h, :], 0.5, 0.5, ALU.mult, ALU.add))
                for i in range(TPH):
                    last = v.tensor_scalar(xs[:, h, i, :], xn[:, h, i, :], weight[:, h, i:i + 1], None, ALU.mult)
                last.then_inc(xs_set, 1)

            def back(n4, pr):
                hold(dve, up_mm, n4 + (pr + 1))
                hold(dve, silu_set, n4 + (pr + 3))
                v.tensor_tensor(hidden[:, pr, :], ps[:, BANK_UP + pr % 2, :], silu[:, pr % 2, :],
                                ALU.mult).then_inc(hidden_set, 1)

            def finish(n, b, h):
                hold(dve, down_mm, n)
                hold(dve, y_out[h], b * 16 + 16)
                v.tensor_tensor(y[:, h, :, :], ps[:, BANK_DOWN, :].rearrange("p (n f) -> p n f", n=TPH),
                                x1_of(b, h), ALU.add).then_inc(y_set, 1)

            dve.sem_inc(hidden_set, 2)
            residual(1, 0, 0)
            route(1, 0)
            residual(2, 0, 1)
            def steps(n4, n, b, h, nb=None, more=True):
                back(n4, 0)
                back(n4, 1)
                if more:
                    route(n + 1, 1 - h)
                back(n4, 2)
                back(n4, 3)
                if nb is not None:
                    residual(n + 2, nb, h)
                finish(n, b, h)

            def two(t):
                for h in range(2):
                    steps(t * 8 + 4 * h, t * 2 + (h + 1), t, h, t + 1)
            two(0)
            dve.wait_ge(sums_in, 16 * BATCH)
            invert(BATCH - 1, BATCH)
            looped(dve, BATCH - 2, lambda t: two(t + 1), 12, chain)
            steps(8 * (BATCH - 1), STEPS - 1, BATCH - 1, 0)
            steps(8 * (BATCH - 1) + 4, STEPS, BATCH - 1, 1, None, False)

        @block.tensor
        def _(pe):
            mm = nc.tensor.matmul
            for s in turned + v_mm:
                pe.sem_inc(s, 1)
            pe.wait_ge(const_set, 5)
            pe.wait_ge(qkv_in, 16 * 5)

            def turn_tiles(src, bank):
                for i in range(TPH):
                    last = nc.tensor.transpose(ps[:, bank, i * P:(i + 1) * P], src[:, i, :], ident[:])
                return last

            def turn1(b, h):
                pe.wait_ge(xn_set[h], b + 1)
                pe.wait_ge(xn_t_set[h], b + 1)
                turn_tiles(xn[:, h], 4 * h).then_inc(turned[h], 1)

            def project_qk(b, h):
                pe.wait_ge(xn_t_set[h], b + 2)
                pe.wait_ge(qk_set[h], b + 1)
                for side in range(2):
                    last = mm(ps[:, 4 * h + 1 + side, :], w_qkv[:, side, :], xn_t[:, h, :], start=True, stop=True)
                last.then_inc(qk_mm[h], 1)

            def project_v(b, h):
                pe.wait_ge(v_set[h], b + 1)
                for i in range(TPH):
                    last = mm(ps[:, 4 * h + 3, i * P:(i + 1) * P], xn_t[:, h, i * P:(i + 1) * P],
                              w_qkv[:, 2, :], start=True, stop=True)
                last.then_inc(v_mm[h], 1)

            turn1(0, 0)
            pe.wait_ge(bv_wide_set, 1)
            mm(ps[:, 7, 0:DIM], xs[:, 0, 0, :], w_o[:], start=True, stop=True).then_inc(bias_mm, 1)
            with pe.Fori(0, BATCH - 1) as t:
                project_qk(t, 0)
                turn1(t, 1)
                project_v(t, 0)
                project_qk(t, 1)
                turn1(t + 1, 0)
                project_v(t, 1)
            project_qk(BATCH - 1, 0)
            turn1(BATCH - 1, 1)
            project_v(BATCH - 1, 0)
            project_qk(BATCH - 1, 1)
            project_v(BATCH - 1, 1)
            for h in range(2):
                pe.wait_ge(qk_set[h], BATCH + 1)
                pe.wait_ge(v_set[h], BATCH + 1)

            def rows_piece(n, k, bank):
                qt, head, k0, cols, _ = PIECES[n]
                return mm(ps[:, 5 + bank, 0:cols], q_rows[:, k, head, qt * P:(qt + 1) * P],
                          k_rows[:, k, head, k0:k0 + cols], start=True, stop=True)

            def turn_top(c, bank):
                bank_b = ps[0:12, 5 + bank, :].bitcast(BF16)
                for i in range(TPH):
                    last = nc.tensor.transpose(bank_b[:, i * P:(i + 1) * P],
                                               top_part[:, c, i].rearrange("p r g -> p (r g)"), ident_b[:])
                return last

            pe.wait_ge(rows_in[0], 112)
            for r, e in enumerate(uses(LEAD)):
                if r >= 3:
                    pe.wait_ge(rot_free, r - 2)
                if e[0] == "turn":
                    pe.wait_ge(top_part_set, 1)
                bank = (r + 1) % 3
                ins = rows_piece(e[1], 0, bank) if e[0] == "piece" else turn_top(0, bank)
                ins.then_inc(rot_mm, 1)

            def step(t, k, rows, between=None):
                nt, nk = (t, k + 1) if k < 2 else (t + 1, 0)
                r = 0
                first_piece = True
                for e in (FULL if rows else TAIL):
                    if e[0] == "scores":
                        i, p = e[1], e[2]
                        c, j, q0, n = SLOTS[i]
                        x0 = 2 * i + p
                        if p == 0 and j == 0:
                            pe.wait_ge(top_in[k][c], t * 16 + 32)
                        pe.wait_ge(exp_done, at(24, t, k, x0 + 1))
                        for s in range(2):
                            last = mm(ps[:, 2 * (x0 % 2) + s, 0:n],
                                      k_rows[:, k, 2 * p + s, j * P:(j + 1) * P],
                                      q_rows[:, k, 2 * p + s, c * HALF + q0:(c + 1) * HALF],
                                      start=True, stop=True)
                        last.then_inc(scores_mm, 1)
                    elif e[0] == "values":
                        i = e[1]
                        c, j, q0, n = SLOTS[i]
                        if i == 0:
                            pe.wait_ge(v_unit_set, at(1, t, k, 1))
                        if j == 0:
                            pe.wait_ge(sum_set, at(2, t, k, c + 1))
                        if i in DIAG:
                            pe.wait_ge(diag_done, at(2 * len(DIAG), t, k, 2 * DIAG.index(i) + 2))
                        else:
                            pe.wait_ge(exp_done, at(24, t, k, 2 + 2 * i + 2))
                        for g in range(GH):
                            last = mm(ps[32 * g:32 * g + 32, BANK_V, q0:HALF], v_unit[:, k, j, g, :],
                                      prob[:, i % 3, g, 0:n], start=(j == 0), stop=(i == LAST[c]))
                        last.then_inc(values_mm, 1)
                        if between:
                            between(i)
                    else:
                        if e[0] == "piece" and first_piece:
                            pe.wait_ge(rows_in[nk], (nt + 1) * 112)
                            first_piece = False
                        if e[0] == "turn":
                            pe.wait_ge(top_part_set, at(2, t, k, 2 if e[1] else 3))
                        pe.wait_ge(rot_free, rot(t, k, rot_before(r) + 1))
                        ins = rows_piece(e[1], nk, r % 3) if e[0] == "piece" else turn_top(e[1], r % 3)
                        ins.then_inc(rot_mm, 1)
                        r += 1

            pe.sem_inc(values_mm, 3)
            with pe.Fori(0, LOOPS) as t:
                for k in range(3):
                    step(t, k, True)
            def project3(n, h):
                pe.wait_ge(attn_set, n)
                for i in range(TPH):
                    last = mm(ps[:, BANK_PROJ, i * P:(i + 1) * P], attn[:, h, i * P:(i + 1) * P], w_o[:],
                              start=True, stop=True)
                last.then_inc(proj_mm, 1)

            def turn_xn(n, h):
                pe.wait_ge(xn3, n)
                turn_tiles(xn[:, h], BANK_TURN).then_inc(xn_turned, 1)

            def logits(n, h):
                pe.wait_ge(xn_t3, n)
                for i in range(TPH):
                    last = mm(ps[:, BANK_ROUTE, i * EXPERTS:(i + 1) * EXPERTS], xn_t[:, h, i * P:(i + 1) * P],
                              w_gate[:], start=True, stop=True)
                last.then_inc(logit_mm, 1)

            def turn_refused(n, h):
                pe.wait_ge(refused_set, n)
                turned_rows = ps[0:EXPERTS, BANK_ROUTE, :].bitcast(BF16)[:, HALF:]
                for i in range(TPH):
                    last = nc.tensor.transpose(turned_rows[:, i * P:(i + 1) * P], refused[:, h, i, :], ident_b[:])
                last.then_inc(refused_turned, 1)

            def turn_xs(n, h):
                pe.wait_ge(xs_set, n)
                turn_tiles(xs[:, h], BANK_TURN).then_inc(xs_turned, 1)

            def back(n, n4, h, pr):
                if pr == 0:
                    pe.wait_ge(xs_t_set, n)
                    pe.wait_ge(refused_t_set, n)
                cols = slice(pr * P, (pr + 1) * P)
                pe.wait_ge(silu_set, n4 + (pr + 1))
                gate = ps[:, BANK_GATE + pr % 2, :]
                mm(gate, w_g[:, cols], xs_t[:, h, :], start=True, stop=False)
                mm(gate, shut[:, cols], refused_t[:], start=False, stop=True).then_inc(gate_mm, 1)
                pe.wait_ge(hidden_set, n4 + (pr + 1))
                mm(ps[:, BANK_UP + pr % 2, :], w_u[:, cols], xs_t[:, h, :], start=True, stop=True
                   ).then_inc(up_mm, 1)

            def down(n, n4):
                pe.wait_ge(hidden_set, n4 + (PAIRS + 2))
                pe.wait_ge(y_set, n)
                for i in range(TPH):
                    for pr in range(PAIRS):
                        last = mm(ps[:, BANK_DOWN, i * P:(i + 1) * P], hidden[:, pr, i * P:(i + 1) * P],
                                  w_d[:, pr, :], start=(pr == 0), stop=(pr == PAIRS - 1))
                last.then_inc(down_mm, 1)

            def lead_in(i):
                if i == FRONT[0]:
                    pe.wait_ge(rot_free, FIRST + ROT * (UNITS - 1) + 1)
                    pe.wait_ge(weights_in, 16 * 4)
                    project3(1, 0)
                if i == FRONT[1]:
                    turn_xn(1, 0)
                if i == FRONT[2]:
                    logits(1, 0)
                    project3(2, 1)

            step(LOOPS, 0, False, lead_in)
            turn_refused(1, 0)
            turn_xs(1, 0)
            pe.wait_ge(exp_done, 24 * UNITS + 2)
            pe.wait_ge(sum_set, 2 * UNITS + 1)

            def steps(n, n4, h, after=True, more=True):
                back(n, n4, h, 0)
                if more:
                    turn_xn(n + 1, 1 - h)
                back(n, n4, h, 1)
                if more:
                    logits(n + 1, 1 - h)
                back(n, n4, h, 2)
                back(n, n4, h, 3)
                if after:
                    project3(n + 2, h)
                if more:
                    turn_refused(n + 1, 1 - h)
                    turn_xs(n + 1, 1 - h)
                down(n, n4)

            with pe.Fori(0, BATCH - 1) as t:
                for h in range(2):
                    steps(t * 2 + (h + 1), t * 8 + 4 * h, h)
            steps(STEPS - 1, 8 * (BATCH - 1), 0, False)
            steps(STEPS, 8 * (BATCH - 1) + 4, 1, False, False)


def kernel(L0_attn_x, L0_attn_Wq, L0_attn_bq, L0_attn_Wk, L0_attn_bk, L0_attn_Wv, L0_attn_bv, L0_attn_Wo,
           L0_attn_bo, L0_ffn_gate_w, L0_ffn_w_gate, L0_ffn_w_up, L0_ffn_w_down):
    import numpy as np
    import concourse.bacc as bacc
    from concourse.bass_utils import run_bass_kernel_spmd

    def t(w):
        return np.ascontiguousarray(np.asarray(w).T)

    def by_unit(w):
        return np.ascontiguousarray(w.reshape(-1, HEADS // GH, GH, HD).transpose(0, 1, 3, 2)).reshape(-1, DIM)

    rows = EXPERTS * INNER
    given = {
        "x": np.asarray(L0_attn_x),
        "wq_t": by_unit(t(L0_attn_Wq)), "wk_t": by_unit(t(L0_attn_Wk)), "wv_t": t(L0_attn_Wv), "wo_t": t(L0_attn_Wo),
        "bq": by_unit(np.asarray(L0_attn_bq)).reshape(DIM, 1), "bk": by_unit(np.asarray(L0_attn_bk)).reshape(DIM, 1),
        "bv": np.asarray(L0_attn_bv).reshape(DIM, 1), "bo": np.asarray(L0_attn_bo).reshape(1, DIM),
        "gate_t": t(L0_ffn_gate_w),
        "wg_t": t(np.asarray(L0_ffn_w_gate).reshape(rows, DIM)),
        "wu_t": t(np.asarray(L0_ffn_w_up).reshape(rows, DIM)),
        "wd_t": np.ascontiguousarray(np.asarray(L0_ffn_w_down).transpose(0, 2, 1)).reshape(rows, DIM),
    }
    nc = bacc.Bacc("TRN2", target_bir_lowering=False, num_devices=1)
    args = [nc.dram_tensor(n, a.shape, FP32, kind="ExternalInput").ap() for n, a in given.items()]
    out = nc.dram_tensor("out", (BATCH, SEQ, DIM), FP32, kind="ExternalOutput").ap()
    layer_kernel(nc, *args, out)
    r = run_bass_kernel_spmd(nc, [given], core_ids=[0])
    return r.results[0]["out"]
```
